# Optimizing a Trainium2 kernel written in Bass

```python
import numpy as np
import jax
import jax.numpy as jnp

def _softmax(x, axis=-1):
    return jax.nn.softmax(x, axis=axis)

def _gelu(x):
    return jax.nn.gelu(x, approximate=True)

def _silu(x):
    return jax.nn.silu(x)

def _sigmoid(x):
    return jax.nn.sigmoid(x)

def _layernorm(x, axis=-1, eps=1e-05):
    m = jnp.mean(x, axis=axis, keepdims=True)
    v = jnp.var(x, axis=axis, keepdims=True)
    return (x - m) / jnp.sqrt(v + eps)

def _scatter_add(tgt, idx, src, axis=0):
    return tgt.at[idx].add(src)

def _segment_sum(src, seg, n):
    return jax.ops.segment_sum(src, seg, n)
kernel_name = 'mk_recurrent_d2_jaxref_r8_69b37c'

def setup_inputs(seed: int=0):
    np.random.seed(seed)
    _w = jnp.asarray

    def _L0_attn_setup():
        import jax, jax.numpy as jnp
        import numpy as np
        B, L, H = (8, 256, 128)
        MASK_IDENTITY = True
        key = jax.random.key(seed)
        ks = jax.random.split(key, 7)
        s = 1.0 / np.sqrt(H)
        return {'x': jax.random.normal(ks[0], (B, L, H), dtype=jnp.float32), 'Wq': jax.random.uniform(ks[1], (H, H), jnp.float32, -s, s), 'bq': jax.random.uniform(ks[2], (H,), jnp.float32, -s, s), 'Wk': jax.random.uniform(ks[3], (H, H), jnp.float32, -s, s), 'bk': jax.random.uniform(ks[4], (H,), jnp.float32, -s, s), 'Wv': jax.random.uniform(ks[5], (H, H), jnp.float32, -s, s), 'bv': jax.random.uniform(ks[6], (H,), jnp.float32, -s, s)}
    _L0_attn_in = _L0_attn_setup()

    def _L0_ffn_setup():
        import jax, jax.numpy as jnp
        import numpy as np
        B, T, D, H, E = (4, 256, 128, 256, 8)
        TOP_K = int(E * 0.25)
        key = jax.random.key(seed)
        ks = jax.random.split(key, 6)
        x = jax.random.normal(ks[0], (B, T, D), dtype=jnp.float32)
        gate = jax.random.normal(ks[1], (D, E), dtype=jnp.float32)
        W1 = jax.random.normal(ks[2], (E, D, H), dtype=jnp.float32) * D ** (-0.5)
        b1 = jnp.zeros((E, H), dtype=jnp.float32)
        W2 = jax.random.normal(ks[3], (E, H, D), dtype=jnp.float32) * H ** (-0.5)
        b2 = jnp.zeros((E, D), dtype=jnp.float32)
        return {'x': x, 'gate': gate, 'W1': W1, 'b1': b1, 'W2': W2, 'b2': b2}
    _L0_ffn_in = _L0_ffn_setup()

    def _L1_attn_setup():
        import jax, jax.numpy as jnp
        import numpy as np
        B, L, D_MODEL = (4, 256, 128)
        EXPAND = 2
        D_INNER = EXPAND * D_MODEL
        D_STATE = 16
        D_CONV = 4
        DT_RANK = (D_MODEL + 15) // 16
        EPS = 1e-05

        def _rmsnorm(x, w):
            return x * jax.lax.rsqrt(jnp.mean(x * x, axis=-1, keepdims=True) + EPS) * w

        def _causal_depthwise_conv(x, w, b):
            xp = jnp.pad(x, ((0, 0), (0, 0), (D_CONV - 1, 0)))
            y = jax.lax.conv_general_dilated(xp, w[:, None, :], window_strides=(1,), padding='VALID', dimension_numbers=('NCH', 'OIH', 'NCH'), feature_group_count=D_INNER)
            return y + b[None, :, None]

        def _selective_scan(u, delta, A, Bm, Cm, D):

            def step(s, inp):
                d_t, B_t, C_t, u_t = inp
                dA = jnp.exp(d_t[..., None] * A)
                dBu = d_t[..., None] * B_t[:, None, :] * u_t[..., None]
                s = s * dA + dBu
                y = jnp.einsum('bds,bs->bd', s, C_t)
                return (s, y)
            s0 = jnp.zeros((u.shape[0], D_INNER, D_STATE), u.dtype)
            xs = (delta.swapaxes(0, 1), Bm.swapaxes(0, 1), Cm.swapaxes(0, 1), u.swapaxes(0, 1))
            _, ys = jax.lax.scan(step, s0, xs)
            return ys.swapaxes(0, 1) + u * D
        key = jax.random.key(seed)
        ks = jax.random.split(key, 10)
        s = 0.02
        return {'x': jax.random.normal(ks[0], (B, L, D_MODEL), jnp.float32), 'norm_w': jnp.ones((D_MODEL,), jnp.float32), 'in_proj_w': jax.random.normal(ks[1], (2 * D_INNER, D_MODEL), jnp.float32) * s, 'conv_w': jax.random.normal(ks[2], (D_INNER, D_CONV), jnp.float32) * s, 'conv_b': jnp.zeros((D_INNER,), jnp.float32), 'x_proj_w': jax.random.normal(ks[3], (DT_RANK + 2 * D_STATE, D_INNER), jnp.float32) * s, 'dt_proj_w': jax.random.normal(ks[4], (D_INNER, DT_RANK), jnp.float32) * s, 'dt_proj_b': jnp.log(jnp.expm1(jnp.full((D_INNER,), 0.01, jnp.float32))), 'A_log': jnp.log(jnp.broadcast_to(jnp.arange(1, D_STATE + 1, dtype=jnp.float32), (D_INNER, D_STATE))), 'D': jnp.ones((D_INNER,), jnp.float32), 'out_proj_w': jax.random.normal(ks[5], (D_MODEL, D_INNER), jnp.float32) * s}
    _L1_attn_in = _L1_attn_setup()

    def _L1_ffn_setup():
        import jax, jax.numpy as jnp
        import numpy as np
        B, S, D, F, E = (1, 128, 128, 512, 8)
        EPS = 1e-05

        def _sublayer(xs, g, b, W1e, b1e, W2e, b2e):
            mu = jnp.mean(xs, axis=-1, keepdims=True)
            var = jnp.mean(jnp.square(xs - mu), axis=-1, keepdims=True)
            h = (xs - mu) * jax.lax.rsqrt(var + EPS) * g + b
            return xs + jax.nn.relu(h @ W1e.T + b1e) @ W2e.T + b2e
        key = jax.random.key(seed)
        ks = jax.random.split(key, 4)
        x = jax.random.normal(ks[0], (B, S, D), jnp.float32)
        centroids = jax.random.normal(ks[1], (E, D), jnp.float32) * 0.1
        gamma = jnp.ones((E, D), jnp.float32)
        beta = jnp.zeros((E, D), jnp.float32)
        W1 = jax.random.normal(ks[2], (E, F, D), jnp.float32) * 0.02
        b1 = jnp.zeros((E, F), jnp.float32)
        W2 = jax.random.normal(ks[3], (E, D, F), jnp.float32) * 0.02
        b2 = jnp.zeros((E, D), jnp.float32)
        return {'x': x, 'centroids': centroids, 'gamma': gamma, 'beta': beta, 'W1': W1, 'b1': b1, 'W2': W2, 'b2': b2}
    _L1_ffn_in = _L1_ffn_setup()
    _d = {'L0_attn_x': _L0_attn_in['x'], 'L0_attn_Wq': _L0_attn_in['Wq'], 'L0_attn_bq': _L0_attn_in['bq'], 'L0_attn_Wk': _L0_attn_in['Wk'], 'L0_attn_bk': _L0_attn_in['bk'], 'L0_attn_Wv': _L0_attn_in['Wv'], 'L0_attn_bv': _L0_attn_in['bv'], 'L0_ffn_gate': _L0_ffn_in['gate'], 'L0_ffn_W1': _L0_ffn_in['W1'], 'L0_ffn_b1': _L0_ffn_in['b1'], 'L0_ffn_W2': _L0_ffn_in['W2'], 'L0_ffn_b2': _L0_ffn_in['b2'], 'L1_attn_norm_w': _L1_attn_in['norm_w'], 'L1_attn_in_proj_w': _L1_attn_in['in_proj_w'], 'L1_attn_conv_w': _L1_attn_in['conv_w'], 'L1_attn_conv_b': _L1_attn_in['conv_b'], 'L1_attn_x_proj_w': _L1_attn_in['x_proj_w'], 'L1_attn_dt_proj_w': _L1_attn_in['dt_proj_w'], 'L1_attn_dt_proj_b': _L1_attn_in['dt_proj_b'], 'L1_attn_A_log': _L1_attn_in['A_log'], 'L1_attn_D': _L1_attn_in['D'], 'L1_attn_out_proj_w': _L1_attn_in['out_proj_w'], 'L1_ffn_centroids': _L1_ffn_in['centroids'], 'L1_ffn_gamma': _L1_ffn_in['gamma'], 'L1_ffn_beta': _L1_ffn_in['beta'], 'L1_ffn_W1': _L1_ffn_in['W1'], 'L1_ffn_b1': _L1_ffn_in['b1'], 'L1_ffn_W2': _L1_ffn_in['W2'], 'L1_ffn_b2': _L1_ffn_in['b2']}
    _x0 = _d['L0_attn_x']
    _d['L0_attn_x'] = jax.random.normal(jax.random.fold_in(jax.random.key(seed), 1), (8, 512, 128), dtype=_x0.dtype)
    del _x0
    return _d

def reference(L0_attn_x, L0_attn_Wq, L0_attn_bq, L0_attn_Wk, L0_attn_bk, L0_attn_Wv, L0_attn_bv, L0_ffn_gate, L0_ffn_W1, L0_ffn_b1, L0_ffn_W2, L0_ffn_b2, L1_attn_norm_w, L1_attn_in_proj_w, L1_attn_conv_w, L1_attn_conv_b, L1_attn_x_proj_w, L1_attn_dt_proj_w, L1_attn_dt_proj_b, L1_attn_A_log, L1_attn_D, L1_attn_out_proj_w, L1_ffn_centroids, L1_ffn_gamma, L1_ffn_beta, L1_ffn_W1, L1_ffn_b1, L1_ffn_W2, L1_ffn_b2):

    def _L0_attn_ref(x, Wq, bq, Wk, bk, Wv, bv):
        import jax, jax.numpy as jnp
        import numpy as np
        B, L, H = (8, 256, 128)
        MASK_IDENTITY = True
        q = jnp.einsum('blh,oh->blo', x, Wq) + bq
        k = jnp.einsum('blh,oh->blo', x, Wk) + bk
        v = jnp.einsum('blh,oh->blo', x, Wv) + bv
        hidden = q.shape[-1]
        attn = jnp.einsum('blh,bmh->blm', q / hidden, k)
        if MASK_IDENTITY:
            mask_value = -jnp.finfo(attn.dtype).max
            eye = jnp.eye(attn.shape[-1], dtype=bool)
            attn = jnp.where(eye[None, :, :], mask_value, attn)
        attn = jax.nn.softmax(attn, axis=-1)
        return jnp.einsum('blm,bmh->blh', attn, v)

    def _L0_ffn_ref(x, gate, W1, b1, W2, b2):
        import jax, jax.numpy as jnp
        import numpy as np
        B, T, D, H, E = (4, 256, 128, 256, 8)
        TOP_K = int(E * 0.25)
        raw_gate = jax.nn.softmax(jnp.einsum('btd,de->bte', x, gate), axis=-1)
        topk_scores, topk_idx = jax.lax.top_k(raw_gate, TOP_K)
        mask = jax.nn.one_hot(topk_idx, E, dtype=raw_gate.dtype).sum(axis=-2)
        gate_topk = mask * raw_gate
        gate_topk = gate_topk / jnp.maximum(gate_topk.sum(axis=-1, keepdims=True), 1e-12)
        h = jax.nn.relu(jnp.einsum('btd,edh->beth', x, W1) + b1[None, :, None, :])
        expert_out = jnp.einsum('beth,ehd->betd', h, W2) + b2[None, :, None, :]
        out = jnp.einsum('bte,betd->btd', gate_topk, expert_out)
        return out

    def _L1_attn_ref(x, norm_w, in_proj_w, conv_w, conv_b, x_proj_w, dt_proj_w, dt_proj_b, A_log, D, out_proj_w):
        import jax, jax.numpy as jnp
        import numpy as np
        B, L, D_MODEL = (4, 256, 128)
        EXPAND = 2
        D_INNER = EXPAND * D_MODEL
        D_STATE = 16
        D_CONV = 4
        DT_RANK = (D_MODEL + 15) // 16
        EPS = 1e-05

        def _rmsnorm(x, w):
            return x * jax.lax.rsqrt(jnp.mean(x * x, axis=-1, keepdims=True) + EPS) * w

        def _causal_depthwise_conv(x, w, b):
            xp = jnp.pad(x, ((0, 0), (0, 0), (D_CONV - 1, 0)))
            y = jax.lax.conv_general_dilated(xp, w[:, None, :], window_strides=(1,), padding='VALID', dimension_numbers=('NCH', 'OIH', 'NCH'), feature_group_count=D_INNER)
            return y + b[None, :, None]

        def _selective_scan(u, delta, A, Bm, Cm, D):

            def step(s, inp):
                d_t, B_t, C_t, u_t = inp
                dA = jnp.exp(d_t[..., None] * A)
                dBu = d_t[..., None] * B_t[:, None, :] * u_t[..., None]
                s = s * dA + dBu
                y = jnp.einsum('bds,bs->bd', s, C_t)
                return (s, y)
            s0 = jnp.zeros((u.shape[0], D_INNER, D_STATE), u.dtype)
            xs = (delta.swapaxes(0, 1), Bm.swapaxes(0, 1), Cm.swapaxes(0, 1), u.swapaxes(0, 1))
            _, ys = jax.lax.scan(step, s0, xs)
            return ys.swapaxes(0, 1) + u * D
        h = _rmsnorm(x, norm_w)
        xz = jnp.einsum('bld,ed->ble', h, in_proj_w)
        xi, z = jnp.split(xz, 2, axis=-1)
        xi = _causal_depthwise_conv(xi.swapaxes(1, 2), conv_w, conv_b).swapaxes(1, 2)
        xi = jax.nn.silu(xi)
        x_dbl = jnp.einsum('bld,ed->ble', xi, x_proj_w)
        dt, Bm, Cm = jnp.split(x_dbl, [DT_RANK, DT_RANK + D_STATE], axis=-1)
        delta = jax.nn.softplus(jnp.einsum('blr,dr->bld', dt, dt_proj_w) + dt_proj_b)
        A = -jnp.exp(A_log)
        y = _selective_scan(xi, delta, A, Bm, Cm, D)
        y = y * jax.nn.silu(z)
        out = jnp.einsum('bld,ed->ble', y, out_proj_w)
        return out + x

    def _L1_ffn_ref(x, centroids, gamma, beta, W1, b1, W2, b2):
        import jax, jax.numpy as jnp
        import numpy as np
        B, S, D, F, E = (1, 128, 128, 512, 8)
        EPS = 1e-05

        def _sublayer(xs, g, b, W1e, b1e, W2e, b2e):
            mu = jnp.mean(xs, axis=-1, keepdims=True)
            var = jnp.mean(jnp.square(xs - mu), axis=-1, keepdims=True)
            h = (xs - mu) * jax.lax.rsqrt(var + EPS) * g + b
            return xs + jax.nn.relu(h @ W1e.T + b1e) @ W2e.T + b2e
        feats = x.reshape(-1, x.shape[-1])
        scores = jax.lax.stop_gradient(feats @ centroids.T)
        expert = jnp.argmax(scores, axis=1)
        onehot = jax.nn.one_hot(expert, E, dtype=feats.dtype)
        alpha = jax.nn.sigmoid(jnp.sum(feats * centroids[expert], axis=-1, keepdims=True))
        ys = jax.vmap(_sublayer, in_axes=(None, 0, 0, 0, 0, 0, 0))(feats, gamma, beta, W1, b1, W2, b2)
        y = jnp.einsum('te,etd->td', onehot, ys)
        out = alpha * y + (1.0 - alpha) * feats
        return out.reshape(x.shape)
    x = L0_attn_x
    xn = _layernorm(x, axis=-1)
    s = _L0_attn_ref(xn, L0_attn_Wq, L0_attn_bq, L0_attn_Wk, L0_attn_bk, L0_attn_Wv, L0_attn_bv)
    g = _silu(_L0_ffn_ref(xn, L0_ffn_gate, L0_ffn_W1, L0_ffn_b1, L0_ffn_W2, L0_ffn_b2))
    x = x + s * g
    xn = _layernorm(x, axis=-1)
    s = _L1_attn_ref(xn, L1_attn_norm_w, L1_attn_in_proj_w, L1_attn_conv_w, L1_attn_conv_b, L1_attn_x_proj_w, L1_attn_dt_proj_w, L1_attn_dt_proj_b, L1_attn_A_log, L1_attn_D, L1_attn_out_proj_w)
    g = _silu(_L1_ffn_ref(xn, L1_ffn_centroids, L1_ffn_gamma, L1_ffn_beta, L1_ffn_W1, L1_ffn_b1, L1_ffn_W2, L1_ffn_b2))
    x = x + s * g
    return x

_drawn_inputs = setup_inputs


def setup_inputs(seed=0):
    import zlib

    import numpy as np

    out = dict(_drawn_inputs(seed))
    spreads = {'L0_ffn_b1': (0.0, 0.8),
     'L0_ffn_b2': (0.0, 0.8),
     'L1_attn_norm_w': (1.0, 0.6),
     'L1_attn_conv_b': (0.0, 0.8),
     'L1_attn_dt_proj_b': (-4.600166320800781, 0.6),
     'L1_attn_D': (1.0, 0.6),
     'L1_ffn_gamma': (1.0, 0.6),
     'L1_ffn_beta': (0.0, 0.8),
     'L1_ffn_b1': (0.0, 0.76),
     'L1_ffn_b2': (0.0, 0.1)}
    factors = {'L0_attn_Wq': 8.0,
     'L0_attn_bq': 8.0,
     'L0_attn_Wk': 8.0,
     'L0_attn_bk': 8.0,
     'L0_attn_Wv': 5.262,
     'L0_ffn_W1': 2.842,
     'L1_attn_in_proj_w': 8.0,
     'L1_attn_conv_w': 8.0,
     'L1_attn_x_proj_w': 8.0,
     'L1_attn_dt_proj_w': 8.0,
     'L1_attn_A_log': 8.0,
     'L1_attn_out_proj_w': 8.0,
     'L1_ffn_W1': 2.706}
    for name, (base, spread) in spreads.items():
        noise = np.random.default_rng([zlib.crc32(name.encode()), seed]).standard_normal(out[name].shape)
        drawn = base * np.exp(spread * noise) if base else spread * noise
        out[name] = jnp.asarray(drawn.astype(out[name].dtype))
    for name, factor in factors.items():
        out[name] = (out[name] * factor).astype(out[name].dtype)
    return out
```

```python
from contextlib import ExitStack

import numpy as np

import concourse.bass as bass
from concourse import mybir

F32 = mybir.dt.float32
BF16 = mybir.dt.bfloat16
ALU = mybir.AluOpType
ACT = mybir.ActivationFunctionType
AX = mybir.AxisListType

NB, T, D = 8, 512, 128
NT = T // 128
E = 8
H0, H1 = 256, 512
NCH = {"A": E * H0 // 128, "F": E * H1 // 128}
DI, NS, TAPS, RANK = 256, 16, 4, 8
NH = DI // 128
STEPS = NS * NH
EPS = 1e-5
LAG = 3
BANKS = 2


def chunk_steps(group):
    per = NCH[group] // E
    out = []
    for c in range(NCH[group] + LAG):
        if c < NCH[group]:
            if c % per == 0:
                out.append(("gb", c // per))
            out.append(("h", c))
        if c >= LAG:
            out.append(("m", c - LAG))
    return out


A_STEPS = ([("ln0", 0), ("xT", 0), ("gl", 0), ("q", 0), ("k", 0), ("v", 0)] + [("s", i) for i in range(NT)]
           + [("gate", 0)] + [("p", i) for i in range(NT)] + [("gT", 0), ("o", 0), ("b2", 0)] + chunk_steps("A")
           + [("silu", 0), ("ft", 0), ("ln1", 0), ("x1T", 0), ("hT", 0)] + [("xi", h) for h in range(NH)]
           + [("z", h) for h in range(NH)] + [("bc", 0), ("dt", 0)] + [("dl", h) for h in range(NH)])
F_STEPS = ([("sc", 0), ("oh", 0), ("b2", 0)] + chunk_steps("F") + [("fe", 0), ("ft", 0), ("silu", 0)])
NO_BANK = {"ln0", "gate", "b2", "m", "silu", "ln1", "fe"}
COST = {"h": 9, "m": 9, "gb": 3, "q": 9, "k": 9, "v": 9, "s": 9, "o": 9, "xi": 9, "z": 9, "bc": 18, "dt": 18,
        "dl": 9, "b2": 9}


def cost(step):
    return COST.get(step[0], 3)


def merged():
    out = []
    for g, steps in (("F", F_STEPS), ("A", A_STEPS)):
        total, at = sum(cost(s) for s in steps), 0
        for s in steps:
            out.append((at / total, g, s))
            at += cost(s)
    out.sort(key=lambda x: x[0])
    return [(g, s) for _, g, s in out]


ORDER = merged()


def slots(groups):
    run = [(g, s) for g, s in ORDER if g in groups]
    total, at = sum(cost(s) for _, s in run), 0
    out = [[] for _ in range(STEPS)]
    for g, s in run:
        out[min(STEPS - 1, at * STEPS // total)].append((g, s))
        at += cost(s)
    return out


JOBS = {g: [s for gg, s in ORDER if gg == g and s[0] not in NO_BANK] for g in "AF"}
JOBS["C"] = [("op", 0)]
BANK = {}
for _g, _s in ORDER:
    if _s[0] not in NO_BANK:
        BANK[_g, _s] = len(BANK) % BANKS
BANK["C", ("op", 0)] = 0
IN_BANK = {g: [[s for s in JOBS[g] if BANK[g, s] == k] for k in range(BANKS)] for g in "AFC"}
LINKS = {("dve", "A"): 60, ("dve", "F"): 10, ("pool", "A"): 24, ("pool", "F"): 4, ("pool", "C"): 4,
         ("act", "A"): 12, ("act", "F"): 4}

CONSTS = {
    "ident": np.eye(128, dtype=np.float32),
    "rowsel": np.tile(np.eye(32, dtype=np.float32), (3, 1)),
    "first": np.tile(np.arange(E, 0, -1, dtype=np.float32), (128, NT, 1)).reshape(128, NT * E),
}


def build(nc, ins, out):
    nc.disable_value_cache = True
    ctx = ExitStack()
    with ctx:
        def sb(name, shape, dt=F32):
            return ctx.enter_context(nc.sbuf_tensor(name, shape, dt))

        def sem(name):
            return ctx.enter_context(nc.semaphore(name))

        W = {}
        for name, (_, shape) in ins.items():
            if name != "x":
                W[name] = sb("w_" + name, shape)
        sel = sb("sel", [96, 32, 128], BF16)
        ident_b = sb("ident_b", [128, 128], BF16)
        mask_b = sb("mask_b", [128, 128], BF16)
        neghalf = sb("neghalf", [128, NT])
        eps = sb("eps", [128, NT])
        bqs = sb("bqs", [128, 1])
        Aneg = sb("Aneg", [128, NH * NS])
        b1f = sb("b1f", [128, NCH["F"]])
        ident = W["ident"]

        x_tok = sb("x_tok", [128, 2, NT, D])
        stats = sb("stats", [128, NT, 6])
        mv = sb("mv", [128, NT, 2])
        ve = sb("ve", [128, NT])
        rstd = sb("rstd", [128, NT])
        xnT = sb("xnT", [128, T])
        qkv = sb("qkv", [128, 5, T])
        qT, kT = qkv[:, 0], qkv[:, 1]
        v_tok, xn_tok, s_tok = (qkv[:, k].rearrange("p (i d) -> p i d", i=NT) for k in (2, 3, 4))
        hT = qkv[:, 1]
        ab, rl = qkv[:, 0:NH], qkv[:, NH:2 * NH]
        nmax = sb("nmax", [128, NT])
        rsum = sb("rsum", [128, NT])
        rs = sb("rs", [128, NT])
        prob = sb("prob", [128, NT, T])
        se = prob[:, 0]
        tmp, ht_tok = (prob[:, k].rearrange("p (i d) -> p i d", i=NT) for k in (1, 2))
        rest = prob[0:96, 3]
        cv, ec = prob[:, 0:NH], prob[:, NH:2 * NH]
        probT = sb("probT", [128, NT, T])
        g0T = probT[:, 0]
        zr, ez = probT[:, 0:NH], probT[:, NH:2 * NH]
        gm = sb("gm", [128, NT])
        gr = sb("gr", [128, NT])
        gt = sb("gt", [128, NT, E])
        gp = sb("gp", [128, NT, E])
        eq = sb("eq", [128, NT, E])
        oh1 = sb("oh1", [128, NT, E])
        oh2 = sb("oh2", [128, NT, E])
        grep = sb("grep", [128, NT, 96])
        gTf = sb("gTf", [E, T])
        g3 = sb("g3", [96, T], BF16)
        midp = sb("midp", [96, T], BF16)
        gbs = {g: sb("gbs" + g, [128, 2, T]) for g in "AF"}
        hid = {g: sb("hid" + g, [128, 4, T]) for g in "AF"}
        q2 = sb("q2", [128, NT])
        rstd2 = sb("rstd2", [128, NT])
        xn1_tok = sb("xn1_tok", [128, 2, NT, D])
        xn1T = sb("xn1T", [128, 2, T])
        xpad = sb("xpad", [128, NH, TAPS - 1 + T])
        u = sb("u", [128, 2, NH, T])
        zg = sb("zg", [128, 2, NH, T])
        bc3 = sb("bc3", [96, 2, T], BF16)
        dt8 = sb("dt8", [RANK, T])
        delta = sb("delta", [128, 2, NH, T])
        du = sb("du", [128, 2, NH, T])
        am = sb("am", [128, NT])
        fm = sb("fm", [128, NT])
        alpha = sb("alpha", [128, NT])
        feq = sb("feq", [128, NT, E])
        ohr = sb("ohr", [128, NT, E])
        ohF = sb("ohF", [E, T])
        ohB = sb("ohB", [E, T], BF16)
        fT = sb("fT", [128, T])
        r1 = fT[:].rearrange("p (i d) -> p i d", i=NT)
        g1 = sb("g1", [128, NT, D])
        dA = sb("dA", [128, 4, T])
        st = sb("st", [128, 4, T])
        Cs = sb("Cs", [128, 2, T])
        ot = sb("ot", [128, NT, D])

        work = [ctx.enter_context(nc.psum_tensor(f"work{k}", [128, T], F32)) for k in range(BANKS)]
        facc = {g: ctx.enter_context(nc.psum_tensor("facc" + g, [128, T], F32)) for g in "AF"}
        yacc = [ctx.enter_context(nc.psum_tensor(f"yacc{h}", [128, T], F32)) for h in range(NH)]
        Bps = ctx.enter_context(nc.psum_tensor("Bps", [128, T], F32))
        Cps = ctx.enter_context(nc.psum_tensor("Cps", [128, T], F32))

        loads = {k: sem("load_" + k) for k in ("small", "ffn0", "mamba", "ffn1")}
        ready = {g: sem("ready" + g) for g in "AFC"}
        free = {g: [sem(f"free{g}{k}") for k in range(BANKS)] for g in "AFC"}
        chain = {k: sem("chain_%s_%s" % k) for k in LINKS}
        prep_act, prep_pe, prep_dve = sem("prep_act"), sem("prep_pe"), sem("prep_dve")
        sig = {n: sem(n) for n in (
            "x_in", "stats", "mean0", "rstd0", "xn0", "smax", "g_in", "g_exp", "g_rep", "g_hi", "g_split", "hot",
            "siluA_e", "g0T", "t_sg", "x1", "mean1", "rstd1", "xn1", "ht",
            "cv", "ec", "ec2", "u", "ez2", "zg", "bc_hi", "bc3", "sp", "du",
            "gatedA", "usedA", "accA", "gatedF", "usedF", "fT",
            "a_exp", "alpha", "r1", "siluF_e", "siluF_r", "g1",
            "B_in", "C_in", "C_out", "dA", "dBu", "scan", "P", "y_add", "y_done",
            "yo", "yg", "s1", "ot", "out")}

        def filled(eng, g, step, b):
            eng.wait_ge(ready[g], b * len(JOBS[g]) + JOBS[g].index(step) + 1)

        def emptied(eng, g, step, b):
            k = BANK[g, step]
            eng.wait_ge(free[g][k], b * len(IN_BANK[g][k]) + IN_BANK[g][k].index(step) + 1)

        def bank_free(eng, g, step, b, groups):
            k = BANK[g, step]
            run = [(gg, s) for gg, s in ORDER if gg in groups and BANK.get((gg, s)) == k]
            at = run.index((g, step))
            if at:
                gg, s = run[at - 1]
                emptied(eng, gg, s, b + (gg == "A") - (g == "A"))
            elif "F" in groups:
                bb = b - (g == "A")
                eng.wait_ge(free["F"][k], bb * len(IN_BANK["F"][k]))
                eng.wait_ge(free["A"][k], (bb + 1) * len(IN_BANK["A"][k]))
                eng.wait_ge(free["C"][k], bb * len(IN_BANK["C"][k]))

        def bank(g, step):
            return work[BANK[g, step]]

        def tiles(ap):
            return ap.rearrange("p (i d) -> p i d", i=NT)

        class Link:

            def __init__(self, eng, who, g, b):
                self.eng, self.key, self.b, self.n = eng, (who, g), b, 0

            def __call__(self, ins):
                self.n += 1
                assert self.n <= LINKS[self.key], self.key
                ins.then_inc(chain[self.key], 1)
                self.eng.wait_ge(chain[self.key], self.b * LINKS[self.key] + self.n)

            def end(self):
                if self.n < LINKS[self.key]:
                    self.eng.sem_inc(chain[self.key], LINKS[self.key] - self.n)

        block = ctx.enter_context(nc.Block())

        LOADS = {"small": ["ident", "rowsel", "first", "wqT", "wkT", "wvT", "bq", "bk", "bv", "gate"],
                 "ffn0": ["w1a", "b1a", "w2a", "b2a"],
                 "mamba": ["norm_w", "winT", "conv_w", "conv_b", "xpBC", "xpDT", "dtpT", "dtb", "alog", "dskip",
                           "woutT"],
                 "ffn1": ["centT", "gammaT", "betaT", "w1f", "b1f_raw", "w2f", "b2f"]}

        @block.sync
        def _(sp):
            sp.dma_start(x_tok[:, 0], ins["x"][0][0].rearrange("(i p) d -> p i d", p=128)).then_inc(sig["x_in"], 16)
            for part, names in LOADS.items():
                for name in names:
                    sp.dma_start(W[name][:], ins[name][0]).then_inc(loads[part], 16)

            def load(b, par):
                if not isinstance(b, int) or b >= 2:
                    sp.wait_ge(sig["ot"], b - 1)
                sp.dma_start(x_tok[:, par], ins["x"][0][b].rearrange("(i p) d -> p i d", p=128)
                             ).then_inc(sig["x_in"], 16)

            def store(b):
                sp.wait_ge(sig["ot"], b + 1)
                sp.dma_start(out[b].rearrange("(i p) d -> p i d", p=128), ot[:]).then_inc(sig["out"], 16)

            load(1, 1)
            store(0)
            load(2, 0)
            with sp.Fori(0, (NB - 4) // 2) as it:
                for par in (1, 0):
                    store(it * 2 + 2 - par)
                    load(it * 2 + 4 - par, par)
            for b in range(NB - 3, NB):
                store(b)
                if b + 2 < NB:
                    load(b + 2, b % 2)
            sp.wait_ge(sig["out"], 16 * NB)

        @block.tensor
        def _(pe):
            mm = nc.tensor.matmul
            pe.wait_ge(loads["small"], 16 * len(LOADS["small"]))
            pe.wait_ge(prep_dve, 1)

            def a_step(step, b, par, groups):
                g = "A"
                name, i = step
                if name not in NO_BANK:
                    bank_free(pe, g, step, b, groups)
                    w = bank(g, step)
                last = None
                if name == "xT":
                    pe.wait_ge(sig["xn0"], b + 1)
                    for t in range(NT):
                        last = nc.tensor.transpose(w[:, t * 128:(t + 1) * 128], xn_tok[:, t], ident[:])
                elif name == "gl":
                    emptied(pe, g, ("xT", 0), b)
                    for t in range(NT):
                        last = mm(w[:, t * E:(t + 1) * E], xnT[:, t * 128:(t + 1) * 128], W["gate"][:],
                                  start=True, stop=True)
                elif name in ("q", "k"):
                    last = mm(w[:], W["wqT" if name == "q" else "wkT"][:], xnT[:], start=True, stop=True)
                elif name == "v":
                    for t in range(NT):
                        last = mm(w[:, t * 128:(t + 1) * 128], xnT[:, t * 128:(t + 1) * 128], W["wvT"][:],
                                  start=True, stop=True)
                elif name == "s":
                    if i == 0:
                        emptied(pe, g, ("q", 0), b)
                        emptied(pe, g, ("k", 0), b)
                    mm(w[:], qT[:, i * 128:(i + 1) * 128], kT, start=True, stop=False)
                    last = mm(w[:, i * 128:(i + 1) * 128], ident_b[:], mask_b[:], start=False, stop=True)
                elif name == "p":
                    if i == 0:
                        for t in range(NT):
                            emptied(pe, g, ("s", t), b)
                    for t in range(NT):
                        last = nc.tensor.transpose(w[:, t * 128:(t + 1) * 128], prob[:, t, i * 128:(i + 1) * 128],
                                                   ident[:])
                elif name == "o":
                    emptied(pe, g, ("v", 0), b)
                    for m in range(NT):
                        emptied(pe, g, ("p", m), b)
                    for t in range(NT):
                        for m in range(NT):
                            last = mm(w[:, t * 128:(t + 1) * 128], probT[:, m, t * 128:(t + 1) * 128], v_tok[:, m],
                                      start=(m == 0), stop=(m == NT - 1))
                elif name == "gT":
                    pe.wait_ge(sig["g_rep"], b + 1)
                    for t in range(NT):
                        last = nc.tensor.transpose(w[0:96, t * 128:(t + 1) * 128], grep[:, t], ident[:])
                elif name == "ft":
                    pe.wait_ge(sig["g0T"], b + 1)
                    for t in range(NT):
                        last = nc.tensor.transpose(w[:, t * 128:(t + 1) * 128], g0T[:, t * 128:(t + 1) * 128], ident[:])
                elif name == "x1T":
                    pe.wait_ge(sig["xn1"], b + 1)
                    for t in range(NT):
                        last = nc.tensor.transpose(w[:, t * 128:(t + 1) * 128], xn1_tok[:, par, t], ident[:])
                elif name == "hT":
                    pe.wait_ge(sig["ht"], b + 1)
                    for t in range(NT):
                        last = nc.tensor.transpose(w[:, t * 128:(t + 1) * 128], ht_tok[:, t], ident[:])
                elif name in ("xi", "z"):
                    if step == ("xi", 0):
                        emptied(pe, g, ("hT", 0), b)
                    c = i + (NH if name == "z" else 0)
                    last = mm(w[:], W["winT"][:, c * 128:(c + 1) * 128], hT, start=True, stop=True)
                elif name in ("bc", "dt"):
                    if name == "bc":
                        pe.wait_ge(sig["u"], NH * (b + 1))
                    rows = 96 if name == "bc" else RANK
                    wt = W["xpBC" if name == "bc" else "xpDT"]
                    for h in range(NH):
                        last = mm(w[0:rows], wt[:, h * rows:(h + 1) * rows], u[:, par, h],
                                  start=(h == 0), stop=(h == NH - 1))
                elif name == "dl":
                    emptied(pe, g, ("dt", 0), b)
                    last = mm(w[:], W["dtpT"][:, i * 128:(i + 1) * 128], dt8[:], start=True, stop=True)
                else:
                    last = expert_step("A", step, b)
                if last is not None and name not in NO_BANK:
                    last.then_inc(ready[g], 1)

            def expert_step(g, step, b):
                name, i = step
                x = xnT[:] if g == "A" else xn1T[:, f_par[0]]
                w1, w2, b2 = (W[n + g.lower()] for n in ("w1", "w2", "b2"))
                gates = gTf if g == "A" else ohF
                if name == "b2":
                    if g == "A":
                        emptied(pe, g, ("gT", 0), b)
                    else:
                        emptied(pe, g, ("oh", 0), b)
                    pe.wait_ge(sig["accA" if g == "A" else "fT"], b)
                    return mm(facc[g][:], b2[:], gates[:], start=True, stop=False)
                if name == "gb":
                    if g == "A":
                        if i == 0:
                            pe.wait_ge(sig["g_split"], b + 1)
                        return mm(bank(g, step)[:], sel[:, i], g3[:], start=True, stop=True)
                    return mm(bank(g, step)[:], sel[0:E, i], ohB[:], start=True, stop=True)
                if name == "h":
                    return mm(bank(g, step)[:], w1[:, i * 128:(i + 1) * 128], x, start=True, stop=True)
                if name == "m":
                    pe.wait_ge(sig["gated" + g], b * NCH[g] + i + 1)
                    return mm(facc[g][:], w2[:, i * 128:(i + 1) * 128], hid[g][:, i % 4],
                              start=False, stop=(i == NCH[g] - 1)).then_inc(sig["used" + g], 1)

            f_par = [0]

            def f_step(step, b, par, groups):
                g = "F"
                name, i = step
                f_par[0] = par
                if name not in NO_BANK:
                    bank_free(pe, g, step, b, groups)
                    w = bank(g, step)
                if name == "sc":
                    emptied(pe, "A", ("x1T", 0), b)
                    for t in range(NT):
                        last = mm(w[:, t * E:(t + 1) * E], xn1T[:, par, t * 128:(t + 1) * 128], W["centT"][:],
                                  start=True, stop=True)
                elif name == "oh":
                    pe.wait_ge(sig["hot"], b + 1)
                    for t in range(NT):
                        last = nc.tensor.transpose(w[0:E, t * 128:(t + 1) * 128], ohr[:, t], ident[:])
                elif name == "ft":
                    pe.wait_ge(sig["fT"], b + 1)
                    for t in range(NT):
                        last = nc.tensor.transpose(w[:, t * 128:(t + 1) * 128], fT[:, t * 128:(t + 1) * 128], ident[:])
                else:
                    last = expert_step("F", step, b)
                if name not in NO_BANK:
                    last.then_inc(ready[g], 1)

            def spread(n, b, par):
                if n == 0:
                    pe.wait_ge(sig["bc3"], b + 1)
                pe.wait_ge(sig["dBu"], b * STEPS + NH * n)
                mm(Bps[:], sel[:, n], bc3[:, par], start=True, stop=True).then_inc(sig["B_in"], 1)
                pe.wait_ge(sig["C_out"], b * NS + n)
                mm(Cps[:], sel[:, NS + n], bc3[:, par], start=True, stop=True).then_inc(sig["C_in"], 1)

            def add_state(s, b):
                n, h = divmod(s, NH)
                if n == 0:
                    pe.wait_ge(sig["y_done"], b * NH)
                pe.wait_ge(sig["P"], b * STEPS + s + 1)
                mm(yacc[h][:], ident[:], st[:, s % 4], start=(n == 0), stop=(n == NS - 1)).then_inc(sig["y_add"], 1)

            def body(groups, b, par):
                if "F" in groups:
                    spread(0, b, par)
                    deal = slots(groups)
                    for s in range(STEPS):
                        if s % NH == 1 and s // NH + 1 < NS:
                            spread(s // NH + 1, b, par)
                        if s >= 3:
                            add_state(s - 3, b)
                        for g, step in deal[s]:
                            if g == "A":
                                a_step(step, b + 1, 1 - par, groups)
                            else:
                                f_step(step, b, par, groups)
                    for s in range(STEPS - 3, STEPS):
                        add_state(s, b)
                    k = BANK["C", ("op", 0)]
                    if "A" in groups:
                        pe.wait_ge(free["A"][k], (b + 2) * len(IN_BANK["A"][k]))
                    pe.wait_ge(free["F"][k], (b + 1) * len(IN_BANK["F"][k]))
                    pe.wait_ge(sig["yg"], b + 1)
                    for t in range(NT):
                        for h in range(NH):
                            last = mm(work[k][:, t * 128:(t + 1) * 128], du[:, par, h, t * 128:(t + 1) * 128],
                                      W["woutT"][:, h * 128:(h + 1) * 128], start=(h == 0), stop=(h == NH - 1))
                    last.then_inc(ready["C"], 1)
                else:
                    for g, step in ORDER:
                        if g == "A":
                            a_step(step, 0, 0, groups)

            pe.wait_ge(loads["ffn1"], 16 * len(LOADS["ffn1"]))
            for c in range(NCH["F"]):
                last = mm(work[0][:, c:c + 1], W["w1f"][:, c * 128:(c + 1) * 128],
                          W["betaT"][:, c // (H1 // 128):c // (H1 // 128) + 1], start=True, stop=True)
            last.then_inc(prep_pe, 1)
            pe.wait_ge(loads["ffn0"], 16 * len(LOADS["ffn0"]))
            pe.wait_ge(loads["mamba"], 16 * len(LOADS["mamba"]))
            pe.wait_ge(prep_dve, 2)
            body("A", -1, 1)
            body("AF", 0, 0)
            with pe.Fori(0, (NB - 2) // 2) as it:
                body("AF", it * 2 + 1, 1)
                body("AF", it * 2 + 2, 0)
            body("F", NB - 1, 1)

        @block.scalar
        def _(act):
            def go(out, in_, func, **k):
                return nc.scalar.activation(out, in_, func, **k)

            def expert_step(g, step, b):
                name, i = step
                per = NCH[g] // E
                if name == "gb":
                    filled(act, g, step, b)
                    act.wait_ge(sig["gated" + g], b * NCH[g] + (i - 1) * per if i >= 2 else b * NCH[g])
                    go(gbs[g][:, i % 2], bank(g, step)[:], ACT.Copy).then_inc(free[g][BANK[g, step]], 1)
                elif name == "h":
                    filled(act, g, step, b)
                    act.wait_ge(sig["used" + g], b * NCH[g] + i - 3 if i >= 4 else b * NCH[g])
                    bias = W["b1a"] if g == "A" else b1f
                    go(hid[g][:, i % 4], bank(g, step)[:], ACT.Relu, bias=bias[:, i:i + 1]
                       ).then_inc(free[g][BANK[g, step]], 1)

            def split_head(g, step, b, dst, signal):
                filled(act, g, step, b)
                go(dst, bank(g, step)[0:96], ACT.Copy).then_inc(sig[signal], 1)

            def a_step(step, b, par):
                g = "A"
                name, i = step
                fr = free[g][BANK[g, step]] if name not in NO_BANK else None
                w = bank(g, step) if name not in NO_BANK else None
                if name in ("gb", "h"):
                    expert_step(g, step, b)
                elif name == "xT":
                    filled(act, g, step, b)
                    act.wait_ge(sig["usedA"], b * NCH["A"])
                    go(xnT[:], w[:], ACT.Copy).then_inc(fr, 1)
                elif name == "gl":
                    act.wait_ge(sig["g_in"], b + 1)
                    go(gp[:], gt[:], ACT.Exp).then_inc(sig["g_exp"], 1)
                elif name == "q":
                    filled(act, g, step, b)
                    go(qT, w[:], ACT.Identity, bias=bqs[:], scale=1.0 / D).then_inc(fr, 1)
                elif name == "k":
                    filled(act, g, step, b)
                    go(kT, w[:], ACT.Identity, bias=W["bk"][:]).then_inc(fr, 1)
                elif name == "s":
                    act.wait_ge(sig["smax"], b * NT + i + 1)
                    go(prob[:, i], w[:], ACT.Exp, bias=nmax[:, i:i + 1], accum_out=rsum[:, i:i + 1]).then_inc(fr, 1)
                elif name == "p":
                    filled(act, g, step, b)
                    go(probT[:, i], w[:], ACT.Copy).then_inc(fr, 1)
                elif name == "gT":
                    filled(act, g, step, b)
                    go(gTf[:], w[0:E], ACT.Copy)
                    go(g3[:], w[0:96], ACT.Copy).then_inc(sig["g_hi"], 1)
                elif name == "silu":
                    act.wait_ge(sig["usedA"], (b + 1) * NCH["A"])
                    go(se, facc[g][:], ACT.Exp, scale=-1.0).then_inc(sig["siluA_e"], 1)
                elif name == "x1T":
                    filled(act, g, step, b)
                    go(xn1T[:, par], w[:], ACT.Copy).then_inc(fr, 1)
                elif name == "hT":
                    filled(act, g, step, b)
                    go(hT, w[:], ACT.Copy).then_inc(fr, 1)
                elif name == "xi":
                    filled(act, g, step, b)
                    go(xpad[:, i, TAPS - 1:], w[:], ACT.Copy).then_inc(fr, 1)
                elif name == "z":
                    filled(act, g, step, b)
                    go(zr[:, i], w[:], ACT.Copy)
                    go(ez[:, i], w[:], ACT.Exp, scale=-1.0).then_inc(fr, 1)
                    act.wait_ge(sig["cv"], b * NH + i + 1)
                    go(ec[:, i], cv[:, i], ACT.Exp, scale=-1.0).then_inc(sig["ec"], 1)
                elif name == "bc":
                    split_head(g, step, b, bc3[:, par], "bc_hi")
                elif name == "dt":
                    filled(act, g, step, b)
                    go(dt8[:], w[0:RANK], ACT.Copy).then_inc(fr, 1)
                elif name == "dl":
                    filled(act, g, step, b)
                    go(rl[:, i], w[:], ACT.Relu, bias=W["dtb"][:, i:i + 1])
                    lk[g](go(ab[:, i], w[:], ACT.Abs, bias=W["dtb"][:, i:i + 1]))
                    lk[g](go(ab[:, i], ab[:, i], ACT.Exp, scale=-1.0))
                    go(cv[:, i], ab[:, i], ACT.Ln, bias=1.0).then_inc(fr, 1)

            lk = {}

            def f_step(step, b, par):
                g = "F"
                name, i = step
                w = bank(g, step) if name not in NO_BANK else None
                if name in ("gb", "h"):
                    expert_step(g, step, b)
                elif name == "sc":
                    act.wait_ge(sig["hot"], b + 1)
                    go(alpha[:], am[:], ACT.Exp, scale=-1.0).then_inc(sig["a_exp"], 1)
                elif name == "oh":
                    filled(act, g, step, b)
                    go(ohF[:], w[0:E], ACT.Copy)
                    go(ohB[:], w[0:E], ACT.Copy).then_inc(free[g][BANK[g, step]], 1)
                elif name == "fe":
                    act.wait_ge(sig["usedF"], (b + 1) * NCH["F"])
                    go(fT[:], facc[g][:], ACT.Copy).then_inc(sig["fT"], 1)
                elif name == "silu":
                    act.wait_ge(sig["r1"], b + 1)
                    go(g1[:], r1, ACT.Exp, scale=-1.0).then_inc(sig["siluF_e"], 1)

            def copy_c(n, b):
                act.wait_ge(sig["C_in"], b * NS + n + 1)
                act.wait_ge(sig["P"], b * STEPS + NH * (n - 1) if n >= 2 else b * STEPS)
                go(Cs[:, n % 2], Cps[:], ACT.Copy).then_inc(sig["C_out"], 1)

            def decay(s, b, par):
                n, h = divmod(s, NH)
                if s == 0:
                    act.wait_ge(sig["du"], NH * (b + 1))
                act.wait_ge(sig["scan"], b * STEPS + s - 3 if s >= 4 else b * STEPS)
                go(dA[:, s % 4], delta[:, par, h], ACT.Exp, scale=Aneg[:, h * NS + n:h * NS + n + 1]
                   ).then_inc(sig["dA"], 1)

            def body(groups, b, par):
                lk["A"] = Link(act, "act", "A", b + 1)
                if "F" in groups:
                    copy_c(0, b)
                    decay(0, b, par)
                    deal = slots(groups)
                    for s in range(STEPS):
                        if s % NH == 1 and s // NH + 1 < NS:
                            copy_c(s // NH + 1, b)
                        if s + 1 < STEPS:
                            decay(s + 1, b, par)
                        for g, step in deal[s]:
                            if g == "A":
                                a_step(step, b + 1, 1 - par)
                            else:
                                f_step(step, b, par)
                else:
                    for g, step in ORDER:
                        if g == "A":
                            a_step(step, 0, 0)
                if "A" in groups:
                    lk["A"].end()

            act.wait_ge(loads["small"], 16 * len(LOADS["small"]))
            act.wait_ge(loads["ffn0"], 16 * len(LOADS["ffn0"]))
            act.wait_ge(loads["mamba"], 16 * len(LOADS["mamba"]))
            act.wait_ge(loads["ffn1"], 16 * len(LOADS["ffn1"]))
            go(bqs[:], W["bq"][:], ACT.Copy, scale=1.0 / D)
            go(Aneg[:], W["alog"][:], ACT.Exp).then_inc(prep_act, 1)
            act.wait_ge(prep_dve, 3)
            body("A", -1, 1)
            body("AF", 0, 0)
            with act.Fori(0, (NB - 2) // 2) as it:
                body("AF", it * 2 + 1, 1)
                body("AF", it * 2 + 2, 0)
            body("F", NB - 1, 1)

        @block.vector
        def _(dve):
            V = nc.vector
            lk = {}

            def spread8(ap):
                return ap.unsqueeze(2).broadcast_to([128, NT, E])

            def moments(g, x, signal):
                for t in range(NT):
                    last = V.bn_stats(stats[:, t], x[:, t])
                lk[g](last)
                dve.sem_inc(sig["stats"], 1)
                for t in range(NT):
                    last = V.bn_aggr(mv[:, t], stats[:, t])
                last.then_inc(sig[signal], 1)

            def first_max(g, p, m, e, hot):
                lk[g](V.tensor_reduce(m[:], p[:], AX.X, ALU.max))
                lk[g](V.tensor_tensor(e[:], p[:], spread8(m[:]), ALU.is_equal))
                lk[g](V.tensor_tensor(e[:], e[:], tiles8(W["first"]), ALU.mult))
                lk[g](V.tensor_reduce(fm[:] if g == "F" else gr[:], e[:], AX.X, ALU.max))
                lk[g](V.tensor_tensor(hot[:], e[:], spread8(fm[:] if g == "F" else gr[:]), ALU.is_equal))

            def tiles8(t):
                return t[:].rearrange("p (i e) -> p i e", e=E)

            def split_rest(g, step, b, dst, head, signal):
                w = bank(g, step)
                dve.wait_ge(sig[head], b + 1)
                k = V.tensor_tensor(rest, w[0:96], dst, ALU.subtract)
                k.then_inc(free[g][BANK[g, step]], 1)
                emptied(dve, g, step, b)
                V.tensor_copy(dst[32:64], rest[32:64])
                lk[g](V.tensor_copy(midp[64:96], rest[64:96]))
                V.tensor_tensor(dst[64:96], rest[64:96], midp[64:96], ALU.subtract).then_inc(sig[signal], 1)

            def a_step(step, b, par):
                g = "A"
                name, i = step
                fr = free[g][BANK[g, step]] if name not in NO_BANK else None
                w = bank(g, step) if name not in NO_BANK else None
                if name == "ln0":
                    dve.wait_ge(sig["x_in"], 16 * (b + 1))
                    moments(g, x_tok[:, par], "mean0")
                    dve.wait_ge(sig["rstd0"], b + 1)
                    for t in range(NT):
                        last = V.tensor_scalar(xn_tok[:, t], x_tok[:, par, t], mv[:, t, 0:1], rstd[:, t:t + 1],
                                               ALU.subtract, ALU.mult)
                    last.then_inc(sig["xn0"], 1)
                elif name == "v":
                    filled(dve, g, step, b)
                    V.tensor_tensor(v_tok, tiles(w[:]), W["bv"][:].unsqueeze(1).broadcast_to([128, NT, D]), ALU.add
                                    ).then_inc(fr, 1)
                elif name == "s":
                    filled(dve, g, step, b)
                    V.tensor_reduce(nmax[:, i:i + 1], w[:], AX.X, ALU.max, negate=True).then_inc(sig["smax"], 1)
                elif name == "gl":
                    filled(dve, g, step, b)
                    wl = w[:, 0:NT * E].rearrange("p (i e) -> p i e", e=E)
                    lk[g](V.tensor_reduce(gm[:], wl, AX.X, ALU.max))
                    V.tensor_tensor(gt[:], wl, spread8(gm[:]), ALU.subtract).then_inc(sig["g_in"], 1)
                    dve.wait_ge(sig["g_in"], b + 1)
                    dve.sem_inc(fr, 1)
                elif name == "gate":
                    dve.wait_ge(sig["g_exp"], b + 1)
                    emptied(dve, g, ("gl", 0), b)
                    lk[g](V.tensor_reduce(gm[:], gp[:], AX.X, ALU.add))
                    lk[g](V.reciprocal(gr[:], gm[:]))
                    lk[g](V.tensor_tensor(gp[:], gp[:], spread8(gr[:]), ALU.mult))
                    first_max(g, gp, gm, eq, oh1)
                    lk[g](V.scalar_tensor_tensor(gt[:], oh1[:], -4.0, gp[:], ALU.mult, ALU.add))
                    first_max(g, gt, gm, eq, oh2)
                    lk[g](V.tensor_tensor(oh1[:], oh1[:], oh2[:], ALU.add))
                    lk[g](V.tensor_tensor(gp[:], gp[:], oh1[:], ALU.mult))
                    lk[g](V.tensor_reduce(gm[:], gp[:], AX.X, ALU.add))
                    lk[g](V.tensor_scalar(gm[:], gm[:], 1e-12, None, ALU.max))
                    lk[g](V.reciprocal(gr[:], gm[:]))
                    for k in range(3):
                        last = V.tensor_tensor(grep[:, :, 32 * k:32 * k + E], gp[:], spread8(gr[:]), ALU.mult)
                    last.then_inc(sig["g_rep"], 1)
                elif name == "gT":
                    split_rest(g, step, b, g3[:], "g_hi", "g_split")
                elif name == "o":
                    filled(dve, g, step, b)
                    lk[g](V.reciprocal(rs[:], rsum[:]))
                    V.tensor_tensor(s_tok, tiles(w[:]), rs[:].unsqueeze(2).broadcast_to([128, NT, D]), ALU.mult
                                    ).then_inc(fr, 1)
                elif name == "h":
                    emptied(dve, g, step, b)
                    emptied(dve, g, ("gb", i // (NCH[g] // E)), b)
                    V.tensor_tensor(hid[g][:, i % 4], hid[g][:, i % 4], gbs[g][:, i // (NCH[g] // E) % 2], ALU.mult
                                    ).then_inc(sig["gatedA"], 1)
                elif name == "silu":
                    dve.wait_ge(sig["siluA_e"], b + 1)
                    lk[g](V.tensor_scalar(se, se, 1.0, None, ALU.add))
                    lk[g](V.reciprocal(se, se))
                    V.tensor_tensor(g0T, facc[g][:], se, ALU.mult).then_inc(sig["g0T"], 1)
                    dve.wait_ge(sig["g0T"], b + 1)
                    dve.sem_inc(sig["accA"], 1)
                elif name == "ft":
                    filled(dve, g, step, b)
                    V.tensor_tensor(tmp, tiles(w[:]), s_tok, ALU.mult).then_inc(fr, 1)
                elif name == "ln1":
                    dve.wait_ge(sig["x1"], b + 1)
                    moments(g, x_tok[:, par], "mean1")
                    dve.wait_ge(sig["rstd1"], b + 1)
                    for t in range(NT):
                        last = V.tensor_scalar(xn1_tok[:, par, t], x_tok[:, par, t], mv[:, t, 0:1], rstd[:, t:t + 1],
                                               ALU.subtract, ALU.mult)
                    last.then_inc(sig["xn1"], 1)
                    dve.wait_ge(sig["xn1"], b + 1)
                    for t in range(NT):
                        last = V.tensor_scalar(ht_tok[:, t], xn1_tok[:, par, t], rstd2[:, t:t + 1], None, ALU.mult)
                    last.then_inc(sig["ht"], 1)
                elif name == "xi":
                    emptied(dve, g, step, b)
                    cw = W["conv_w"]
                    lk[g](V.tensor_scalar(cv[:, i], xpad[:, i, 0:T], cw[:, i * TAPS:i * TAPS + 1],
                                          W["conv_b"][:, i:i + 1], ALU.mult, ALU.add))
                    for k in range(1, TAPS):
                        last = V.scalar_tensor_tensor(cv[:, i], xpad[:, i, k:k + T],
                                                      cw[:, i * TAPS + k:i * TAPS + k + 1], cv[:, i],
                                                      ALU.mult, ALU.add)
                        if k < TAPS - 1:
                            lk[g](last)
                    last.then_inc(sig["cv"], 1)
                elif name == "z":
                    dve.wait_ge(sig["ec"], b * NH + i + 1)
                    lk[g](V.tensor_scalar(ec[:, i], ec[:, i], 1.0, None, ALU.add))
                    V.reciprocal(ec[:, i], ec[:, i]).then_inc(sig["ec2"], 1)
                    emptied(dve, g, step, b)
                    lk[g](V.tensor_scalar(ez[:, i], ez[:, i], 1.0, None, ALU.add))
                    V.reciprocal(ez[:, i], ez[:, i]).then_inc(sig["ez2"], 1)
                elif name == "bc":
                    split_rest(g, step, b, bc3[:, par], "bc_hi", "bc3")

            def f_step(step, b, par):
                g = "F"
                name, i = step
                w = bank(g, step) if name not in NO_BANK else None
                if name == "sc":
                    filled(dve, g, step, b)
                    wl = w[:, 0:NT * E].rearrange("p (i e) -> p i e", e=E)
                    first_max(g, wl, am, feq, ohr)
                    dve.sem_inc(sig["hot"], 1)
                    dve.sem_inc(free[g][BANK[g, step]], 1)
                    dve.wait_ge(sig["a_exp"], b + 1)
                    lk[g](V.tensor_scalar(alpha[:], alpha[:], 1.0, None, ALU.add))
                    V.reciprocal(alpha[:], alpha[:]).then_inc(sig["alpha"], 1)
                elif name == "ft":
                    filled(dve, g, step, b)
                    dve.wait_ge(sig["alpha"], b + 1)
                    for t in range(NT):
                        last = V.scalar_tensor_tensor(r1[:, t], w[:, t * 128:(t + 1) * 128], alpha[:, t:t + 1],
                                                      xn1_tok[:, par, t], ALU.mult, ALU.add)
                    last.then_inc(sig["r1"], 1)
                    dve.wait_ge(sig["r1"], b + 1)
                    dve.sem_inc(free[g][BANK[g, step]], 1)
                elif name == "silu":
                    dve.wait_ge(sig["siluF_e"], b + 1)
                    lk[g](V.tensor_scalar(g1[:], g1[:], 1.0, None, ALU.add))
                    V.reciprocal(g1[:], g1[:]).then_inc(sig["siluF_r"], 1)

            def scan_input(s, b, par):
                n, h = divmod(s, NH)
                if s == 0:
                    dve.wait_ge(sig["du"], NH * (b + 1))
                if h == 0:
                    dve.wait_ge(sig["B_in"], b * NS + n + 1)
                dve.wait_ge(sig["y_add"], b * STEPS + s - 3 if s >= 4 else b * STEPS)
                V.tensor_tensor(st[:, s % 4], Bps[:], du[:, par, h], ALU.mult).then_inc(sig["dBu"], 1)

            def scan(s, b):
                dve.wait_ge(sig["dA"], b * STEPS + s + 1)
                dve.wait_ge(sig["dBu"], b * STEPS + s + 1)
                V.tensor_tensor_scan(st[:, s % 4], dA[:, s % 4], st[:, s % 4], 0.0, ALU.mult, ALU.add
                                     ).then_inc(sig["scan"], 1)

            def body(groups, b, par):
                lk["A"], lk["F"] = Link(dve, "dve", "A", b + 1), Link(dve, "dve", "F", b)
                if "F" in groups:
                    scan_input(0, b, par)
                    deal = slots(groups)
                    for s in range(STEPS):
                        if s + 1 < STEPS:
                            scan_input(s + 1, b, par)
                        scan(s, b)
                        for g, step in deal[s]:
                            if g == "A":
                                a_step(step, b + 1, 1 - par)
                            else:
                                f_step(step, b, par)
                    dve.wait_ge(sig["y_add"], (b + 1) * STEPS)
                    dve.wait_ge(ready["C"], b)
                    for h in range(NH):
                        V.scalar_tensor_tensor(du[:, par, h], u[:, par, h], W["dskip"][:, h:h + 1], yacc[h][:],
                                               ALU.mult, ALU.add).then_inc(sig["y_done"], 1)
                    dve.wait_ge(ready["C"], b + 1)
                    dve.wait_ge(sig["out"], 16 * b)
                    V.tensor_tensor(ot[:], tiles(work[BANK["C", ("op", 0)]][:]), xn1_tok[:, par], ALU.add
                                    ).then_inc(free["C"][BANK["C", ("op", 0)]], 1)
                else:
                    for g, step in ORDER:
                        if g == "A":
                            a_step(step, 0, 0)
                if "A" in groups:
                    lk["A"].end()
                if "F" in groups:
                    lk["F"].end()

            V.memset(neghalf[:], -0.5)
            V.memset(eps[:], EPS)
            V.memset(grep[:], 0.0)
            V.memset(xpad[:], 0.0)
            dve.wait_ge(loads["small"], 16 * len(LOADS["small"]))
            V.tensor_copy(sel[:], W["rowsel"][:].unsqueeze(2).broadcast_to([96, 32, 128]))
            V.tensor_copy(ident_b[:], ident[:])
            V.tensor_scalar(mask_b[:], ident[:], -(2.0 ** 126), None, ALU.mult).then_inc(prep_dve, 1)
            dve.wait_ge(loads["mamba"], 16 * len(LOADS["mamba"]))
            V.tensor_scalar(W["winT"][:], W["winT"][:], W["norm_w"][:], None, ALU.mult)
            dve.wait_ge(loads["ffn1"], 16 * len(LOADS["ffn1"]))
            dve.wait_ge(prep_pe, 1)
            V.tensor_tensor(b1f[:], work[0][:, 0:NCH["F"]], W["b1f_raw"][:], ALU.add)
            for e in range(E):
                last = V.tensor_scalar(W["w1f"][:, e * H1:(e + 1) * H1], W["w1f"][:, e * H1:(e + 1) * H1],
                                       W["gammaT"][:, e:e + 1], None, ALU.mult)
            last.then_inc(prep_dve, 1)
            dve.wait_ge(prep_act, 1)
            V.tensor_scalar(Aneg[:], Aneg[:], -1.0, None, ALU.mult).then_inc(prep_dve, 1)
            body("A", -1, 1)
            body("AF", 0, 0)
            with dve.Fori(0, (NB - 2) // 2) as it:
                body("AF", it * 2 + 1, 1)
                body("AF", it * 2 + 2, 0)
            body("F", NB - 1, 1)

        @block.gpsimd
        def _(pool):
            G = nc.gpsimd
            lk = {}

            def a_step(step, b, par):
                g = "A"
                name, i = step
                if name in ("ln0", "ln1"):
                    k = name[2]
                    pool.wait_ge(sig["mean" + k], b + 1)
                    lk[g](G.tensor_tensor(ve[:], mv[:, :, 1], eps[:], ALU.add))
                    last = G.tensor_tensor(rstd[:], ve[:], neghalf[:], ALU.pow)
                    if name == "ln0":
                        last.then_inc(sig["rstd0"], 1)
                    else:
                        lk[g](last)
                        lk[g](G.tensor_tensor(q2[:], rstd[:], rstd[:], ALU.mult))
                        lk[g](G.tensor_tensor(q2[:], q2[:], mv[:, :, 1], ALU.mult))
                        lk[g](G.tensor_tensor(q2[:], q2[:], eps[:], ALU.add))
                        G.tensor_tensor(rstd2[:], q2[:], neghalf[:], ALU.pow).then_inc(sig["rstd1"], 1)
                elif name == "ft":
                    emptied(pool, g, step, b)
                    G.tensor_tensor(x_tok[:, par], x_tok[:, par], tmp, ALU.add).then_inc(sig["x1"], 1)
                elif name == "z":
                    pool.wait_ge(sig["ec2"], b * NH + i + 1)
                    G.tensor_tensor(u[:, par, i], cv[:, i], ec[:, i], ALU.mult).then_inc(sig["u"], 1)
                    pool.wait_ge(sig["ez2"], b * NH + i + 1)
                    G.tensor_tensor(zg[:, par, i], zr[:, i], ez[:, i], ALU.mult).then_inc(sig["zg"], 1)
                elif name == "dl":
                    emptied(pool, g, step, b)
                    d = delta[:, par, i]
                    G.tensor_tensor(d, rl[:, i], cv[:, i], ALU.add)
                    lk[g](G.tensor_scalar(ez[:, i], ab[:, i], 1.0, -1.0, ALU.add, ALU.add))
                    lk[g](G.tensor_tensor(ez[:, i], ab[:, i], ez[:, i], ALU.subtract))
                    lk[g](G.tensor_tensor(d, d, ez[:, i], ALU.add))
                    G.tensor_tensor(du[:, par, i], d, u[:, par, i], ALU.mult).then_inc(sig["du"], 1)

            def f_step(step, b, par):
                g = "F"
                name, i = step
                if name == "h":
                    emptied(pool, g, step, b)
                    emptied(pool, g, ("gb", i // (NCH[g] // E)), b)
                    G.tensor_tensor(hid[g][:, i % 4], hid[g][:, i % 4], gbs[g][:, i // (NCH[g] // E) % 2], ALU.mult
                                    ).then_inc(sig["gatedF"], 1)
                elif name == "silu":
                    pool.wait_ge(sig["siluF_r"], b + 1)
                    G.tensor_tensor(g1[:], g1[:], r1, ALU.mult).then_inc(sig["g1"], 1)

            def times_c(s, b):
                n, h = divmod(s, NH)
                if h == 0:
                    pool.wait_ge(sig["C_out"], b * NS + n + 1)
                pool.wait_ge(sig["scan"], b * STEPS + s + 1)
                G.tensor_tensor(st[:, s % 4], st[:, s % 4], Cs[:, n % 2], ALU.mult).then_inc(sig["P"], 1)

            def body(groups, b, par):
                lk["A"], lk["C"] = Link(pool, "pool", "A", b + 1), Link(pool, "pool", "C", b)
                if "F" in groups:
                    deal = slots(groups)
                    for s in range(STEPS):
                        times_c(s, b)
                        for g, step in deal[s]:
                            if g == "A":
                                a_step(step, b + 1, 1 - par)
                            else:
                                f_step(step, b, par)
                    pool.wait_ge(sig["y_done"], NH * (b + 1))
                    pool.wait_ge(sig["zg"], NH * (b + 1))
                    G.tensor_tensor(du[:, par], du[:, par], zg[:, par], ALU.mult).then_inc(sig["yg"], 1)
                    pool.wait_ge(sig["g1"], b + 1)
                    pool.wait_ge(free["C"][BANK["C", ("op", 0)]], b + 1)
                    lk["C"](G.tensor_tensor(ot[:], ot[:], g1[:], ALU.mult))
                    G.tensor_tensor(ot[:], ot[:], x_tok[:, par], ALU.add).then_inc(sig["ot"], 1)
                else:
                    for g, step in ORDER:
                        if g == "A":
                            a_step(step, 0, 0)
                if "A" in groups:
                    lk["A"].end()
                if "F" in groups:
                    lk["C"].end()

            body("A", -1, 1)
            body("AF", 0, 0)
            with pool.Fori(0, (NB - 2) // 2) as it:
                body("AF", it * 2 + 1, 1)
                body("AF", it * 2 + 2, 0)
            body("F", NB - 1, 1)


def layouts(i):
    def halves(a):
        return a.reshape(NH, 128, -1).transpose(1, 0, 2).reshape(128, -1)

    xp = i["L1_attn_x_proj_w"]
    bcrows = xp[RANK:]
    bc3 = np.concatenate([bcrows] * 3, 0).T
    col = lambda a: a.reshape(-1, 128).T
    return {
        "x": i["L0_attn_x"],
        **CONSTS,
        "wqT": i["L0_attn_Wq"].T, "wkT": i["L0_attn_Wk"].T, "wvT": i["L0_attn_Wv"].T,
        "bq": col(i["L0_attn_bq"]), "bk": col(i["L0_attn_bk"]),
        "bv": np.broadcast_to(i["L0_attn_bv"], (128, D)),
        "gate": i["L0_ffn_gate"],
        "w1a": i["L0_ffn_W1"].transpose(1, 0, 2).reshape(D, -1),
        "b1a": col(i["L0_ffn_b1"]),
        "w2a": i["L0_ffn_W2"].reshape(-1, 128, D).transpose(1, 0, 2).reshape(128, -1),
        "b2a": i["L0_ffn_b2"],
        "norm_w": col(i["L1_attn_norm_w"]),
        "winT": i["L1_attn_in_proj_w"].T,
        "conv_w": halves(i["L1_attn_conv_w"]), "conv_b": col(i["L1_attn_conv_b"]),
        "xpBC": halves(bc3), "xpDT": halves(xp[:RANK].T),
        "dtpT": i["L1_attn_dt_proj_w"].T, "dtb": col(i["L1_attn_dt_proj_b"]),
        "alog": halves(i["L1_attn_A_log"]), "dskip": col(i["L1_attn_D"]),
        "woutT": halves(i["L1_attn_out_proj_w"].T),
        "centT": i["L1_ffn_centroids"].T, "gammaT": i["L1_ffn_gamma"].T, "betaT": i["L1_ffn_beta"].T,
        "w1f": i["L1_ffn_W1"].transpose(2, 0, 1).reshape(D, -1),
        "b1f_raw": col(i["L1_ffn_b1"]),
        "w2f": i["L1_ffn_W2"].reshape(E, D, H1 // 128, 128).transpose(3, 0, 2, 1).reshape(128, -1),
        "b2f": i["L1_ffn_b2"],
    }


def kernel(**inputs):
    import concourse.bacc as _bacc
    from concourse.bass_utils import run_bass_kernel_spmd as _run

    nc = _bacc.Bacc("TRN2", target_bir_lowering=False, num_devices=1)
    arrays, ins = {}, {}
    for name, a in layouts({k: np.asarray(v) for k, v in inputs.items()}).items():
        a = np.ascontiguousarray(a)
        arrays[f"in_{name}_dram"] = a
        t = nc.dram_tensor(f"in_{name}_dram", a.shape, mybir.dt.from_np(a.dtype), kind="ExternalInput")
        ins[name] = (t.ap(), list(a.shape))
    out = nc.dram_tensor("out_dram", (NB, T, D), F32, kind="ExternalOutput").ap()
    build(nc, ins, out)
    r = _run(nc, [arrays], core_ids=[0])
    return r.results[0]["out_dram"]
```

```python
from contextlib import ExitStack

import numpy as np

import concourse.bass as bass
from concourse import mybir

F32 = mybir.dt.float32
BF16 = mybir.dt.bfloat16
ALU = mybir.AluOpType
ACT = mybir.ActivationFunctionType
AX = mybir.AxisListType

NB, T, D = 8, 512, 128
SUM_LAG = 2
NT = T // 128
E = 8
H0, H1 = 256, 512
NCH = {"A": E * H0 // 128, "F": E * H1 // 128}
DI, NS, TAPS, RANK = 256, 16, 4, 8
NH = DI // 128
STEPS = NS * NH
EPS = 1e-5
LAG = 3
BANKS = 4


def chunk_steps(group):
    per = NCH[group] // E
    out = []
    for c in range(NCH[group] + LAG):
        if c < NCH[group]:
            if c % per == 0:
                out.append(("gb", c // per))
            out.append(("h", c))
        if c >= LAG:
            out.append(("m", c - LAG))
    return out


def at(group, start, end, steps):
    return [(start + (end - start) * k / len(steps), group, s) for k, s in enumerate(steps)]


def each(name, n):
    return [(name, i) for i in range(n)]


PLACES = (
    at("C", 0.0, 0.01, [("y", 0)]) + at("C", 0.06, 0.07, [("op", 0)])
    + at("A", 0.01, 0.02, [("ln0", 0)]) + at("A", 0.05, 0.06, [("xT", 0)])
    + at("A", 0.075, 0.12, [("gl", 0), ("q", 0), ("k", 0), ("v", 0)])
    + at("A", 0.11, 0.12, [("gate", 0)]) + at("A", 0.13, 0.19, each("s", NT)) + at("A", 0.165, 0.17, [("gT", 0)])
    + at("A", 0.19, 0.20, [("b2", 0)]) + at("A", 0.22, 0.27, each("p", NT)) + at("A", 0.30, 0.31, [("o", 0)])
    + at("A", 0.20, 0.58, chunk_steps("A"))
    + at("A", 0.60, 0.61, [("silu", 0)]) + at("A", 0.64, 0.65, [("ft", 0)]) + at("A", 0.66, 0.67, [("ln1", 0)])
    + at("A", 0.71, 0.73, [("x1T", 0), ("hT", 0)]) + at("A", 0.74, 0.80, each("xi", NH) + each("z", NH))
    + at("A", 0.87, 0.88, [("bc", 0)]) + at("A", 0.90, 0.93, each("dl", NH))
    + at("F", 0.015, 0.02, [("sc", 0)]) + at("F", 0.055, 0.056, [("oh", 0)]) + at("F", 0.075, 0.08, [("b2", 0)])
    + at("F", 0.08, 0.90, chunk_steps("F"))
    + at("F", 0.91, 0.92, [("fe", 0)]) + at("F", 0.94, 0.95, [("ft", 0)]) + at("F", 0.965, 0.97, [("silu", 0)]))
PLACES.sort(key=lambda x: x[0])
ORDER = [(g, s) for _, g, s in PLACES]
NO_BANK = {"ln0", "gate", "b2", "m", "silu", "ln1", "fe", "y"}
AHEAD = {"A": 1, "F": 0, "C": -1}


def slots(groups):
    return [[(g, s) for t, g, s in PLACES if g in groups and int(t * STEPS) == k] for k in range(STEPS)]


JOBS = {g: [s for gg, s in ORDER if gg == g and s[0] not in NO_BANK] for g in "AFC"}
BANK = {}
for _g, _s in ORDER:
    if _s[0] not in NO_BANK:
        BANK[_g, _s] = len(BANK) % BANKS
IN_BANK = {g: [[s for s in JOBS[g] if BANK[g, s] == k] for k in range(BANKS)] for g in "AFC"}
LINKS = {("dve", "A"): 60, ("dve", "F"): 10, ("dve", "C"): 8, ("pool", "A"): 24, ("act", "A"): 12}


class Batch:

    def __init__(self, eng, reg, plus, products=None):
        self.eng, self.reg, self.plus = eng, reg, plus
        self.products = {1: reg} if products is None else products

    def __add__(self, n):
        return Batch(self.eng, self.reg, self.plus + n, self.products)

    def of(self, k, more=0):
        if self.reg is None:
            return self.plus * k + more
        if k not in self.products:
            self.products[k] = self.eng.snap(self.reg * k)
        return self.products[k] + (self.plus * k + more)

    def is_(self, n):
        return self.reg is None and self.plus == n

CONSTS = {
    "ident": np.eye(128, dtype=np.float32),
    "rowsel": np.tile(np.eye(32, dtype=np.float32), (3, 1)),
    "first": np.tile(np.arange(E, 0, -1, dtype=np.float32), (128, NT, 1)).reshape(128, NT * E),
}


def build(nc, ins, out):
    nc.disable_value_cache = True
    ctx = ExitStack()
    with ctx:
        def sb(name, shape, dt=F32):
            return ctx.enter_context(nc.sbuf_tensor(name, shape, dt))

        def sem(name):
            return ctx.enter_context(nc.semaphore(name))

        W = {}
        for name, (_, shape) in ins.items():
            if name != "x":
                W[name] = sb("w_" + name, [128, shape[1]] if name == "dtpT" else shape)
        sel = sb("sel", [96, 32, 128], BF16)
        ident_b = sb("ident_b", [128, 128], BF16)
        mask_b = sb("mask_b", [128, 128], BF16)
        neghalf = sb("neghalf", [128, NT])
        eps = sb("eps", [128, NT])
        bqs = sb("bqs", [128, 1])
        Aneg = sb("Aneg", [128, NH * NS])
        ident = W["ident"]
        b1f = W["b1f_raw"]

        x_in = sb("x_in", [128, NT, D])
        x_tok = sb("x_tok", [128, 2, NT, D])
        stats = sb("stats", [128, NT, 6])
        mv = sb("mv", [128, NT, 2])
        ve = sb("ve", [128, NT])
        rstd = sb("rstd", [128, NT])
        xnT = sb("xnT", [128, T])
        qkv = sb("qkv", [128, 5, T])
        qT, kT = qkv[:, 0], qkv[:, 1]
        v_tok, xn_tok, s_tok = (qkv[:, k].rearrange("p (i d) -> p i d", i=NT) for k in (2, 3, 4))
        hT = qkv[:, 1]
        ab, rl = qkv[:, 0:NH], qkv[:, NH:2 * NH]
        nmax = sb("nmax", [128, NT])
        rsum = sb("rsum", [128, NT])
        rs = sb("rs", [128, NT])
        prob = sb("prob", [128, NT, T])
        se = prob[:, 0]
        tmp, ht_tok = (prob[:, k].rearrange("p (i d) -> p i d", i=NT) for k in (1, 2))
        rest = prob[0:96, 3]
        cv, ec = prob[:, 0:NH], prob[:, NH:2 * NH]
        probT = sb("probT", [128, NT, T])
        g0T = probT[:, 0]
        zr, ez = probT[:, 0:NH], probT[:, NH:2 * NH]
        gm = sb("gm", [128, NT])
        gr = sb("gr", [128, NT])
        gt = sb("gt", [128, NT, E])
        gp = sb("gp", [128, NT, E])
        eq = sb("eq", [128, NT, E])
        oh1 = sb("oh1", [128, NT, E])
        oh2 = sb("oh2", [128, NT, E])
        grep = sb("grep", [128, NT, 96])
        gTf = sb("gTf", [E, T])
        g3 = sb("g3", [96, T], BF16)
        midp = sb("midp", [96, T], BF16)
        gbs = {g: sb("gbs" + g, [128, 2, T]) for g in "AF"}
        hid = {g: sb("hid" + g, [128, 4, T]) for g in "AF"}
        q2 = sb("q2", [128, NT])
        rstd2 = sb("rstd2", [128, NT])
        xn1_tok = sb("xn1_tok", [128, 2, NT, D])
        xn1T = sb("xn1T", [128, 2, T])
        xpad = sb("xpad", [128, NH, TAPS - 1 + T])
        u = sb("u", [128, 2, NH, T])
        zg = sb("zg", [128, 2, NH, T])
        bc3 = sb("bc3", [96, 2, T], BF16)
        dt8 = sb("dt8", [128, T])
        delta = sb("delta", [128, 2, NH, T])
        du = sb("du", [128, 2, NH, T])
        am = sb("am", [128, NT])
        fm = sb("fm", [128, NT])
        alpha = sb("alpha", [128, NT])
        feq = sb("feq", [128, NT, E])
        ohr = sb("ohr", [128, NT, E])
        ohF = gTf
        ohB = sb("ohB", [E, T], BF16)
        fT = sb("fT", [128, T])
        r1 = fT[:].rearrange("p (i d) -> p i d", i=NT)
        g1 = sb("g1", [128, NT, D])
        dA = sb("dA", [128, 2, T])
        st = sb("st", [128, 4, T])
        Cs = sb("Cs", [128, 2, T])
        y = sb("y", [128, NH, T])
        ot = sb("ot", [128, NT, D])

        work = [ctx.enter_context(nc.psum_tensor(f"work{k}", [128, T], F32)) for k in range(BANKS)]
        facc = {g: ctx.enter_context(nc.psum_tensor("facc" + g, [128, T], F32)) for g in "AF"}
        Bps = ctx.enter_context(nc.psum_tensor("Bps", [128, T], F32))
        Cps = ctx.enter_context(nc.psum_tensor("Cps", [128, T], F32))

        loads = {k: sem("load_" + k) for k in ("small", "ffn0", "mamba", "ffn1")}
        ready = {g: sem("ready" + g) for g in "AFC"}
        free = {g: [sem(f"free{g}{k}") for k in range(BANKS)] for g in "AFC"}
        chain = {k: sem("chain_%s_%s" % k) for k in LINKS}
        prep_act, prep_pe, prep_dve = sem("prep_act"), sem("prep_pe"), sem("prep_dve")
        sig = {n: sem(n) for n in (
            "x_in", "stats", "mean0", "rstd0", "xn0", "smax", "g_in", "g_exp", "g_rep", "g_hi", "g_split", "hot",
            "siluA_e", "g0T", "x1", "mean1", "rstd1", "xn1", "ht", "cv", "ec", "u", "zg", "bc_hi", "bc3",
            "sp", "e_kept", "du", "gatedA", "usedA", "gatedF", "usedF", "fT", "a_exp", "alpha", "r1", "siluF_e",
            "g1", "B_in", "C_in", "C_out", "dA", "dBu", "scan", "P", "y_sum", "yo", "s1", "ot", "out")}

        def since(eng, semaphore, value):
            if not isinstance(value, int) or value > 0:
                eng.wait_ge(semaphore, value)

        def filled(eng, g, step, b):
            eng.wait_ge(ready[g], b.of(len(JOBS[g]), JOBS[g].index(step) + 1))

        def emptied(eng, g, step, b):
            k = BANK[g, step]
            eng.wait_ge(free[g][k], b.of(len(IN_BANK[g][k]), IN_BANK[g][k].index(step) + 1))

        def bank_free(eng, g, step, it, groups):
            k = BANK[g, step]

            def jobs_of(present):
                return [(gg, s) for gg, s in ORDER if gg in present and BANK.get((gg, s)) == k]

            run = jobs_of(groups)
            at = run.index((g, step))
            if at:
                gg, s = run[at - 1]
                emptied(eng, gg, s, it + AHEAD[gg])
            elif not it.is_(-1):
                gg, s = jobs_of("A" if it.is_(0) else "FC" if it.is_(NB) else "AF")[-1]
                emptied(eng, gg, s, it + (AHEAD[gg] - 1))

        def bank(g, step):
            return work[BANK[g, step]]

        def tiles(ap):
            return ap.rearrange("p (i d) -> p i d", i=NT)

        class Link:

            def __init__(self, eng, who, g, b):
                self.eng, self.key, self.b, self.n = eng, (who, g), b, 0

            def __call__(self, ins):
                self.n += 1
                assert self.n <= LINKS[self.key], self.key
                ins.then_inc(chain[self.key], 1)
                self.eng.wait_ge(chain[self.key], self.b.of(LINKS[self.key], self.n))

            def end(self):
                if self.n < LINKS[self.key]:
                    self.eng.sem_inc(chain[self.key], LINKS[self.key] - self.n)

        def run(eng, body, between=None):
            const = Batch(eng, None, 0)
            body(const + -1, 1, "A")
            if between:
                between()
            body(const, 0, "AF")
            with eng.Fori(1, NB - 1, 2) as reg:
                it = Batch(eng, reg, 0)
                body(it, 1, "AFC")
                body(it + 1, 0, "AFC")
            body(const + (NB - 1), 1, "FC")
            body(const + NB, 0, "C")

        block = ctx.enter_context(nc.Block())

        LOADS = {"small": ["ident", "rowsel", "first", "wqT", "wkT", "wvT", "bq", "bk", "bv", "gate"],
                 "ffn0": ["w1a", "b1a", "w2a", "b2a"],
                 "mamba": ["norm_w", "winT", "conv_w", "conv_b", "xpBC", "dtpT", "dtb", "alog", "dskip",
                           "woutT"],
                 "ffn1": ["centT", "gammaT", "betaT", "w1f", "b1f_raw", "w2f", "b2f"]}

        @block.sync
        def _(sp):
            def load(b):
                sp.dma_start(x_in[:], ins["x"][0][b.of(1)].rearrange("(i p) d -> p i d", p=128)
                             ).then_inc(sig["x_in"], 16)

            def store(b):
                sp.wait_ge(sig["ot"], b.of(1, 1))
                sp.dma_start(out[b.of(1)].rearrange("(i p) d -> p i d", p=128), ot[:]).then_inc(sig["out"], 16)

            first = Batch(sp, None, 0)
            load(first)
            for part, names in LOADS.items():
                for name in names:
                    sp.dma_start(W[name][96:96 + RANK] if name == "dtpT" else W[name][:], ins[name][0]).then_inc(loads[part], 16)
            sp.wait_ge(sig["x1"], 1)
            load(first + 1)
            sp.wait_ge(sig["x1"], 2)
            load(first + 2)
            with sp.Fori(1, NB - 2) as reg:
                it = Batch(sp, reg, 0)
                store(it + -1)
                sp.wait_ge(sig["x1"], it.of(1, 2))
                load(it + 2)
            for b in range(NB - 3, NB):
                store(first + b)
            sp.wait_ge(sig["out"], 16 * NB)

        @block.tensor
        def _(pe):
            mm = nc.tensor.matmul
            pe.wait_ge(loads["small"], 16 * len(LOADS["small"]))
            pe.wait_ge(prep_dve, 1)

            def a_step(step, it, par, groups):
                b = it + 1
                g = "A"
                name, i = step
                if name not in NO_BANK:
                    bank_free(pe, g, step, it, groups)
                    w = bank(g, step)
                last = None
                if name == "xT":
                    pe.wait_ge(sig["xn0"], b.of(1, 1))
                    for t in range(NT):
                        last = nc.tensor.transpose(w[:, t * 128:(t + 1) * 128], xn_tok[:, t], ident[:])
                elif name == "gl":
                    emptied(pe, g, ("xT", 0), b)
                    for t in range(NT):
                        last = mm(w[:, t * E:(t + 1) * E], xnT[:, t * 128:(t + 1) * 128], W["gate"][:],
                                  start=True, stop=True)
                elif name in ("q", "k"):
                    last = mm(w[:], W["wqT" if name == "q" else "wkT"][:], xnT[:], start=True, stop=True)
                elif name == "v":
                    for t in range(NT):
                        last = mm(w[:, t * 128:(t + 1) * 128], xnT[:, t * 128:(t + 1) * 128], W["wvT"][:],
                                  start=True, stop=True)
                elif name == "s":
                    if i == 0:
                        emptied(pe, g, ("q", 0), b)
                        emptied(pe, g, ("k", 0), b)
                    mm(w[:], qT[:, i * 128:(i + 1) * 128], kT, start=True, stop=False)
                    last = mm(w[:, i * 128:(i + 1) * 128], ident_b[:], mask_b[:], start=False, stop=True)
                elif name == "p":
                    if i == 0:
                        for t in range(NT):
                            emptied(pe, g, ("s", t), b)
                    for t in range(NT):
                        last = nc.tensor.transpose(w[:, t * 128:(t + 1) * 128], prob[:, t, i * 128:(i + 1) * 128],
                                                   ident[:])
                elif name == "o":
                    emptied(pe, g, ("v", 0), b)
                    for m in range(NT):
                        emptied(pe, g, ("p", m), b)
                    for t in range(NT):
                        for m in range(NT):
                            last = mm(w[:, t * 128:(t + 1) * 128], probT[:, m, t * 128:(t + 1) * 128], v_tok[:, m],
                                      start=(m == 0), stop=(m == NT - 1))
                elif name == "gT":
                    pe.wait_ge(sig["g_rep"], b.of(1, 1))
                    for t in range(NT):
                        last = nc.tensor.transpose(w[0:96, t * 128:(t + 1) * 128], grep[:, t], ident[:])
                elif name == "ft":
                    pe.wait_ge(sig["g0T"], b.of(1, 1))
                    for t in range(NT):
                        last = nc.tensor.transpose(w[:, t * 128:(t + 1) * 128], g0T[:, t * 128:(t + 1) * 128], ident[:])
                elif name == "x1T":
                    pe.wait_ge(sig["xn1"], b.of(1, 1))
                    for t in range(NT):
                        last = nc.tensor.transpose(w[:, t * 128:(t + 1) * 128], xn1_tok[:, par, t], ident[:])
                elif name == "hT":
                    pe.wait_ge(sig["ht"], b.of(1, 1))
                    for t in range(NT):
                        last = nc.tensor.transpose(w[:, t * 128:(t + 1) * 128], ht_tok[:, t], ident[:])
                elif name in ("xi", "z"):
                    if step == ("xi", 0):
                        emptied(pe, g, ("hT", 0), b)
                        if it.is_(-1):
                            pe.wait_ge(loads["mamba"], 16 * len(LOADS["mamba"]))
                            pe.wait_ge(prep_dve, 2)
                    c = i + (NH if name == "z" else 0)
                    last = mm(w[:], W["winT"][:, c * 128:(c + 1) * 128], hT, start=True, stop=True)
                elif name == "bc":
                    pe.wait_ge(sig["u"], b.of(NH, NH))
                    rows = 96 + RANK
                    for h in range(NH):
                        last = mm(w[0:rows], W["xpBC"][:, h * rows:(h + 1) * rows], u[:, par, h],
                                  start=(h == 0), stop=(h == NH - 1))
                elif name == "dl":
                    emptied(pe, g, ("bc", 0), b)
                    last = mm(w[:], W["dtpT"][96:96 + RANK, i * 128:(i + 1) * 128], dt8[96:96 + RANK],
                              start=True, stop=True)
                else:
                    last = expert_step("A", step, b)
                if last is not None and name not in NO_BANK:
                    last.then_inc(ready[g], 1)

            def expert_step(g, step, b):
                name, i = step
                x = xnT[:] if g == "A" else xn1T[:, f_par[0]]
                w1, w2, b2 = (W[n + g.lower()] for n in ("w1", "w2", "b2"))
                gates = gTf if g == "A" else ohF
                if name == "b2":
                    if g == "A":
                        emptied(pe, g, ("gT", 0), b)
                    else:
                        emptied(pe, g, ("oh", 0), b)
                    since(pe, sig["g0T" if g == "A" else "fT"], b.of(1))
                    if g == "A" and b.is_(0):
                        pe.wait_ge(loads["ffn0"], 16 * len(LOADS["ffn0"]))
                    return mm(facc[g][:], b2[:], gates[:], start=True, stop=False)
                if name == "gb":
                    if g == "A":
                        if i == 0:
                            pe.wait_ge(sig["g_split"], b.of(1, 1))
                        return mm(bank(g, step)[:], sel[:, i], g3[:], start=True, stop=True)
                    return mm(bank(g, step)[:], sel[0:E, i], ohB[:], start=True, stop=True)
                if name == "h":
                    return mm(bank(g, step)[:], w1[:, i * 128:(i + 1) * 128], x, start=True, stop=True)
                if name == "m":
                    pe.wait_ge(sig["gated" + g], b.of(NCH[g], i + 1))
                    return mm(facc[g][:], w2[:, i * 128:(i + 1) * 128], hid[g][:, i % 4],
                              start=False, stop=(i == NCH[g] - 1)).then_inc(sig["used" + g], 1)

            f_par = [0]

            def f_step(step, it, par, groups):
                b = it
                g = "F"
                name, i = step
                f_par[0] = par
                if name not in NO_BANK:
                    bank_free(pe, g, step, it, groups)
                    w = bank(g, step)
                if name == "sc":
                    emptied(pe, "A", ("x1T", 0), b)
                    for t in range(NT):
                        last = mm(w[:, t * E:(t + 1) * E], xn1T[:, par, t * 128:(t + 1) * 128], W["centT"][:],
                                  start=True, stop=True)
                elif name == "oh":
                    pe.wait_ge(sig["hot"], b.of(1, 1))
                    for t in range(NT):
                        last = nc.tensor.transpose(w[0:E, t * 128:(t + 1) * 128], ohr[:, t], ident[:])
                elif name == "ft":
                    pe.wait_ge(sig["fT"], b.of(1, 1))
                    for t in range(NT):
                        last = nc.tensor.transpose(w[:, t * 128:(t + 1) * 128], fT[:, t * 128:(t + 1) * 128], ident[:])
                else:
                    last = expert_step("F", step, b)
                if name not in NO_BANK:
                    last.then_inc(ready[g], 1)

            def spread(n, b, par):
                if n == 0:
                    pe.wait_ge(sig["bc3"], b.of(1, 1))
                since(pe, sig["dBu"], b.of(STEPS, NH * n))
                mm(Bps[:], sel[:, n], bc3[:, par], start=True, stop=True).then_inc(sig["B_in"], 1)
                since(pe, sig["C_out"], b.of(NS, n))
                mm(Cps[:], sel[:, NS + n], bc3[:, par], start=True, stop=True).then_inc(sig["C_in"], 1)

            def project(it, groups):
                b, par = it + -1, 1 - f_par[0]
                bank_free(pe, "C", ("op", 0), it, groups)
                pe.wait_ge(sig["yo"], b.of(1, 1))
                for t in range(NT):
                    for h in range(NH):
                        last = mm(bank("C", ("op", 0))[:, t * 128:(t + 1) * 128], du[:, par, h, t * 128:(t + 1) * 128],
                                  W["woutT"][:, h * 128:(h + 1) * 128], start=(h == 0), stop=(h == NH - 1))
                last.then_inc(ready["C"], 1)

            def do(g, step, it, par, groups):
                if g == "A":
                    a_step(step, it, 1 - par, groups)
                elif g == "F":
                    f_step(step, it, par, groups)
                elif step[0] == "op":
                    project(it, groups)

            def body(it, par, groups):
                f_par[0] = par
                if "F" not in groups:
                    for g, step in ORDER:
                        if g in groups:
                            do(g, step, it, par, groups)
                    return
                spread(0, it, par)
                deal = slots(groups)
                for s in range(STEPS):
                    if s % NH == 1 and s // NH + 1 < NS:
                        spread(s // NH + 1, it, par)
                    for g, step in deal[s]:
                        do(g, step, it, par, groups)

            def prepare():
                pe.wait_ge(loads["ffn1"], 16 * len(LOADS["ffn1"]))
                for c in range(NCH["F"]):
                    last = mm(facc["F"][:, c:c + 1], W["w1f"][:, c * 128:(c + 1) * 128],
                              W["betaT"][:, c // (H1 // 128):c // (H1 // 128) + 1], start=True, stop=True)
                last.then_inc(prep_pe, 1)
                pe.wait_ge(prep_dve, 3)

            run(pe, body, prepare)

        @block.scalar
        def _(act):
            def go(out, in_, func, **k):
                return nc.scalar.activation(out, in_, func, **k)

            def expert_step(g, step, b):
                name, i = step
                per = NCH[g] // E
                if name == "gb":
                    filled(act, g, step, b)
                    since(act, sig["gated" + g], b.of(NCH[g], (i - 1) * per if i >= 2 else 0))
                    go(gbs[g][:, i % 2], bank(g, step)[:], ACT.Copy).then_inc(free[g][BANK[g, step]], 1)
                elif name == "h":
                    filled(act, g, step, b)
                    since(act, sig["used" + g], b.of(NCH[g], i - 3 if i >= 4 else 0))
                    bias = W["b1a"] if g == "A" else b1f
                    go(hid[g][:, i % 4], bank(g, step)[:], ACT.Relu, bias=bias[:, i:i + 1]
                       ).then_inc(free[g][BANK[g, step]], 1)

            def a_step(step, b, par):
                g = "A"
                name, i = step
                fr = free[g][BANK[g, step]] if name not in NO_BANK else None
                w = bank(g, step) if name not in NO_BANK else None
                if name in ("gb", "h"):
                    expert_step(g, step, b)
                elif name == "xT":
                    filled(act, g, step, b)
                    since(act, sig["usedA"], b.of(NCH["A"]))
                    go(xnT[:], w[:], ACT.Copy).then_inc(fr, 1)
                elif name == "gl":
                    act.wait_ge(sig["g_in"], b.of(1, 1))
                    go(gp[:], gt[:], ACT.Exp).then_inc(sig["g_exp"], 1)
                elif name == "q":
                    filled(act, g, step, b)
                    go(qT, w[:], ACT.Identity, bias=bqs[:], scale=1.0 / D).then_inc(fr, 1)
                elif name == "k":
                    filled(act, g, step, b)
                    go(kT, w[:], ACT.Identity, bias=W["bk"][:]).then_inc(fr, 1)
                elif name == "s":
                    act.wait_ge(sig["smax"], b.of(NT, i + 1))
                    go(prob[:, i], w[:], ACT.Exp, bias=nmax[:, i:i + 1], accum_out=rsum[:, i:i + 1]).then_inc(fr, 1)
                elif name == "p":
                    filled(act, g, step, b)
                    go(probT[:, i], w[:], ACT.Copy).then_inc(fr, 1)
                elif name == "gT":
                    filled(act, g, step, b)
                    go(gTf[:], w[0:E], ACT.Copy)
                    go(g3[:], w[0:96], ACT.Copy).then_inc(sig["g_hi"], 1)
                elif name == "silu":
                    act.wait_ge(sig["usedA"], b.of(NCH["A"], NCH["A"]))
                    go(se, facc[g][:], ACT.Tanh, scale=0.5).then_inc(sig["siluA_e"], 1)
                elif name == "x1T":
                    filled(act, g, step, b)
                    go(xn1T[:, par], w[:], ACT.Copy).then_inc(fr, 1)
                elif name == "hT":
                    filled(act, g, step, b)
                    go(hT, w[:], ACT.Copy).then_inc(fr, 1)
                elif name == "xi":
                    filled(act, g, step, b)
                    go(xpad[:, i, TAPS - 1:], w[:], ACT.Copy).then_inc(fr, 1)
                elif name == "z":
                    filled(act, g, step, b)
                    go(zr[:, i], w[:], ACT.Copy, scale=0.5)
                    go(ez[:, i], w[:], ACT.Tanh, scale=0.5).then_inc(fr, 1)
                    act.wait_ge(sig["cv"], b.of(NH, i + 1))
                    go(ec[:, i], cv[:, i], ACT.Tanh).then_inc(sig["ec"], 1)
                elif name == "bc":
                    filled(act, g, step, b)
                    go(dt8[96:96 + RANK], w[96:96 + RANK], ACT.Copy)
                    go(bc3[:, par], w[0:96], ACT.Copy).then_inc(sig["bc_hi"], 1)
                elif name == "dl":
                    filled(act, g, step, b)
                    go(rl[:, i], w[:], ACT.Relu, bias=W["dtb"][:, i:i + 1])
                    go(ab[:, i], w[:], ACT.Abs, bias=W["dtb"][:, i:i + 1]).then_inc(fr, 1)
                    emptied(act, g, step, b)
                    lk[g](go(ab[:, i], ab[:, i], ACT.Exp, scale=-1.0))
                    if i == NH - 1:
                        go(cv, ab, ACT.Ln, bias=1.0).then_inc(sig["sp"], 1)

            lk = {}

            def f_step(step, b, par):
                g = "F"
                name, i = step
                w = bank(g, step) if name not in NO_BANK else None
                if name in ("gb", "h"):
                    expert_step(g, step, b)
                elif name == "sc":
                    act.wait_ge(sig["hot"], b.of(1, 1))
                    go(alpha[:], am[:], ACT.Exp, scale=-1.0).then_inc(sig["a_exp"], 1)
                elif name == "oh":
                    filled(act, g, step, b)
                    go(ohF[:], w[0:E], ACT.Copy)
                    go(ohB[:], w[0:E], ACT.Copy).then_inc(free[g][BANK[g, step]], 1)
                elif name == "fe":
                    act.wait_ge(sig["usedF"], b.of(NCH["F"], NCH["F"]))
                    go(fT[:], facc[g][:], ACT.Copy).then_inc(sig["fT"], 1)
                elif name == "silu":
                    act.wait_ge(sig["r1"], b.of(1, 1))
                    go(g1[:], r1, ACT.Tanh, scale=0.5).then_inc(sig["siluF_e"], 1)

            def copy_c(n, b):
                act.wait_ge(sig["C_in"], b.of(NS, n + 1))
                since(act, sig["P"], b.of(STEPS, NH * (n - 1)))
                go(Cs[:, n % 2], Cps[:], ACT.Copy).then_inc(sig["C_out"], 1)

            def decay(s, b, par):
                n, h = divmod(s, NH)
                if s == 0:
                    act.wait_ge(sig["du"], b.of(1, 1))
                since(act, sig["scan"], b.of(STEPS, s - 1))
                go(dA[:, s % 2], delta[:, par, h], ACT.Exp, scale=Aneg[:, h * NS + n:h * NS + n + 1]
                   ).then_inc(sig["dA"], 1)

            def do(g, step, it, par):
                if g == "A":
                    a_step(step, it + 1, 1 - par)
                elif g == "F":
                    f_step(step, it, par)

            def body(it, par, groups):
                lk["A"] = Link(act, "act", "A", it + 1)
                if "F" in groups:
                    copy_c(0, it)
                    decay(0, it, par)
                    deal = slots(groups)
                    for s in range(STEPS):
                        if s % NH == 1 and s // NH + 1 < NS:
                            copy_c(s // NH + 1, it)
                        if s + 1 < STEPS:
                            decay(s + 1, it, par)
                        for g, step in deal[s]:
                            do(g, step, it, par)
                else:
                    for g, step in ORDER:
                        if g in groups:
                            do(g, step, it, par)
                if "A" in groups:
                    lk["A"].end()

            def prepare():
                act.wait_ge(prep_dve, 4)

            act.wait_ge(loads["small"], 16 * len(LOADS["small"]))
            go(bqs[:], W["bq"][:], ACT.Copy, scale=1.0 / D)
            act.wait_ge(loads["mamba"], 16 * len(LOADS["mamba"]))
            act.wait_ge(loads["ffn0"], 16 * len(LOADS["ffn0"]))
            go(Aneg[:], W["alog"][:], ACT.Exp).then_inc(prep_act, 1)
            run(act, body, prepare)

        @block.vector
        def _(dve):
            V = nc.vector
            lk = {}

            def spread8(ap):
                return ap.unsqueeze(2).broadcast_to([128, NT, E])

            def moments(g, x, signal):
                for t in range(NT):
                    last = V.bn_stats(stats[:, t], x[:, t])
                lk[g](last)
                dve.sem_inc(sig["stats"], 1)
                for t in range(NT):
                    last = V.bn_aggr(mv[:, t], stats[:, t])
                last.then_inc(sig[signal], 1)

            def first_max(g, p, m, e, hot):
                lk[g](V.tensor_reduce(m[:], p[:], AX.X, ALU.max))
                lk[g](V.tensor_tensor(e[:], p[:], spread8(m[:]), ALU.is_equal))
                lk[g](V.tensor_tensor(e[:], e[:], tiles8(W["first"]), ALU.mult))
                lk[g](V.tensor_reduce(fm[:] if g == "F" else gr[:], e[:], AX.X, ALU.max))
                lk[g](V.tensor_tensor(hot[:], e[:], spread8(fm[:] if g == "F" else gr[:]), ALU.is_equal))

            def tiles8(t):
                return t[:].rearrange("p (i e) -> p i e", e=E)

            def split_rest(g, step, b, dst, head, signal):
                w = bank(g, step)
                dve.wait_ge(sig[head], b.of(1, 1))
                k = V.tensor_tensor(rest, w[0:96], dst, ALU.subtract)
                k.then_inc(free[g][BANK[g, step]], 1)
                emptied(dve, g, step, b)
                V.tensor_copy(dst[32:64], rest[32:64])
                lk[g](V.tensor_copy(midp[64:96], rest[64:96]))
                V.tensor_tensor(dst[64:96], rest[64:96], midp[64:96], ALU.subtract).then_inc(sig[signal], 1)

            def a_step(step, b, par):
                g = "A"
                name, i = step
                fr = free[g][BANK[g, step]] if name not in NO_BANK else None
                w = bank(g, step) if name not in NO_BANK else None
                if name == "ln0":
                    dve.wait_ge(sig["x_in"], b.of(16, 16))
                    moments(g, x_in, "mean0")
                    dve.wait_ge(sig["rstd0"], b.of(1, 1))
                    for t in range(NT):
                        last = V.tensor_scalar(xn_tok[:, t], x_in[:, t], mv[:, t, 0:1], rstd[:, t:t + 1],
                                               ALU.subtract, ALU.mult)
                    last.then_inc(sig["xn0"], 1)
                elif name == "v":
                    filled(dve, g, step, b)
                    V.tensor_tensor(v_tok, tiles(w[:]), W["bv"][:].unsqueeze(1).broadcast_to([128, NT, D]), ALU.add
                                    ).then_inc(fr, 1)
                elif name == "s":
                    filled(dve, g, step, b)
                    V.tensor_reduce(nmax[:, i:i + 1], w[:], AX.X, ALU.max, negate=True).then_inc(sig["smax"], 1)
                elif name == "gl":
                    filled(dve, g, step, b)
                    wl = w[:, 0:NT * E].rearrange("p (i e) -> p i e", e=E)
                    lk[g](V.tensor_reduce(gm[:], wl, AX.X, ALU.max))
                    V.tensor_tensor(gt[:], wl, spread8(gm[:]), ALU.subtract).then_inc(sig["g_in"], 1)
                    dve.wait_ge(sig["g_in"], b.of(1, 1))
                    dve.sem_inc(fr, 1)
                elif name == "gate":
                    dve.wait_ge(sig["g_exp"], b.of(1, 1))
                    emptied(dve, g, ("gl", 0), b)
                    lk[g](V.tensor_reduce(gm[:], gp[:], AX.X, ALU.add))
                    lk[g](V.reciprocal(gr[:], gm[:]))
                    lk[g](V.tensor_tensor(gp[:], gp[:], spread8(gr[:]), ALU.mult))
                    first_max(g, gp, gm, eq, oh1)
                    lk[g](V.scalar_tensor_tensor(gt[:], oh1[:], -4.0, gp[:], ALU.mult, ALU.add))
                    first_max(g, gt, gm, eq, oh2)
                    lk[g](V.tensor_tensor(oh1[:], oh1[:], oh2[:], ALU.add))
                    lk[g](V.tensor_tensor(gp[:], gp[:], oh1[:], ALU.mult))
                    lk[g](V.tensor_reduce(gm[:], gp[:], AX.X, ALU.add))
                    lk[g](V.tensor_scalar(gm[:], gm[:], 1e-12, None, ALU.max))
                    lk[g](V.reciprocal(gr[:], gm[:]))
                    for k in range(3):
                        last = V.tensor_tensor(grep[:, :, 32 * k:32 * k + E], gp[:], spread8(gr[:]), ALU.mult)
                    last.then_inc(sig["g_rep"], 1)
                elif name == "gT":
                    split_rest(g, step, b, g3[:], "g_hi", "g_split")
                elif name == "o":
                    filled(dve, g, step, b)
                    lk[g](V.reciprocal(rs[:], rsum[:]))
                    V.tensor_tensor(s_tok, tiles(w[:]), rs[:].unsqueeze(2).broadcast_to([128, NT, D]), ALU.mult
                                    ).then_inc(fr, 1)
                elif name == "h":
                    emptied(dve, g, step, b)
                    emptied(dve, g, ("gb", i // (NCH[g] // E)), b)
                    V.tensor_tensor(hid[g][:, i % 4], hid[g][:, i % 4], gbs[g][:, i // (NCH[g] // E) % 2], ALU.mult
                                    ).then_inc(sig["gatedA"], 1)
                elif name == "silu":
                    dve.wait_ge(sig["siluA_e"], b.of(1, 1))
                    V.scalar_tensor_tensor(g0T, se, 1.0, facc[g][:], ALU.add, ALU.mult).then_inc(sig["g0T"], 1)
                elif name == "ft":
                    filled(dve, g, step, b)
                    V.scalar_tensor_tensor(tmp, tiles(w[:]), 0.5, s_tok, ALU.mult, ALU.mult).then_inc(fr, 1)
                elif name == "ln1":
                    dve.wait_ge(sig["x1"], b.of(1, 1))
                    moments(g, x_tok[:, par], "mean1")
                    dve.wait_ge(sig["rstd1"], b.of(1, 1))
                    for t in range(NT):
                        last = V.tensor_scalar(xn1_tok[:, par, t], x_tok[:, par, t], mv[:, t, 0:1], rstd[:, t:t + 1],
                                               ALU.subtract, ALU.mult)
                    last.then_inc(sig["xn1"], 1)
                    dve.wait_ge(sig["xn1"], b.of(1, 1))
                    for t in range(NT):
                        last = V.tensor_scalar(ht_tok[:, t], xn1_tok[:, par, t], rstd2[:, t:t + 1], None, ALU.mult)
                    last.then_inc(sig["ht"], 1)
                elif name == "xi":
                    emptied(dve, g, step, b)
                    cw = W["conv_w"]
                    lk[g](V.tensor_scalar(cv[:, i], xpad[:, i, 0:T], cw[:, i * TAPS:i * TAPS + 1],
                                          W["conv_b"][:, i:i + 1], ALU.mult, ALU.add))
                    for k in range(1, TAPS):
                        last = V.scalar_tensor_tensor(cv[:, i], xpad[:, i, k:k + T],
                                                      cw[:, i * TAPS + k:i * TAPS + k + 1], cv[:, i],
                                                      ALU.mult, ALU.add)
                        if k < TAPS - 1:
                            lk[g](last)
                    last.then_inc(sig["cv"], 1)
                elif name == "z":
                    dve.wait_ge(sig["ec"], b.of(NH, i + 1))
                    V.scalar_tensor_tensor(u[:, par, i], ec[:, i], 1.0, cv[:, i], ALU.add, ALU.mult
                                           ).then_inc(sig["u"], 1)
                    emptied(dve, g, step, b)
                    V.scalar_tensor_tensor(zg[:, par, i], ez[:, i], 1.0, zr[:, i], ALU.add, ALU.mult
                                           ).then_inc(sig["zg"], 1)
                elif name == "bc":
                    split_rest(g, step, b, bc3[:, par], "bc_hi", "bc3")
                elif name == "dl" and i == NH - 1:
                    dve.wait_ge(sig["sp"], b.of(1, 1))
                    V.tensor_scalar(ez, ab, 1.0, -1.0, ALU.add, ALU.add).then_inc(sig["e_kept"], 1)

            def f_step(step, b, par):
                g = "F"
                name, i = step
                w = bank(g, step) if name not in NO_BANK else None
                if name == "sc":
                    filled(dve, g, step, b)
                    wl = w[:, 0:NT * E].rearrange("p (i e) -> p i e", e=E)
                    first_max(g, wl, am, feq, ohr)
                    dve.sem_inc(sig["hot"], 1)
                    dve.sem_inc(free[g][BANK[g, step]], 1)
                    dve.wait_ge(sig["a_exp"], b.of(1, 1))
                    lk[g](V.tensor_scalar(alpha[:], alpha[:], 1.0, None, ALU.add))
                    V.reciprocal(alpha[:], alpha[:]).then_inc(sig["alpha"], 1)
                elif name == "ft":
                    filled(dve, g, step, b)
                    dve.wait_ge(sig["alpha"], b.of(1, 1))
                    for t in range(NT):
                        last = V.scalar_tensor_tensor(r1[:, t], w[:, t * 128:(t + 1) * 128], alpha[:, t:t + 1],
                                                      xn1_tok[:, par, t], ALU.mult, ALU.add)
                    last.then_inc(sig["r1"], 1)
                    dve.wait_ge(sig["r1"], b.of(1, 1))
                    dve.sem_inc(free[g][BANK[g, step]], 1)
                elif name == "silu":
                    dve.wait_ge(sig["siluF_e"], b.of(1, 1))
                    V.scalar_tensor_tensor(g1[:], g1[:], 1.0, r1, ALU.add, ALU.mult).then_inc(sig["g1"], 1)

            def scan_input(s, b, par):
                n, h = divmod(s, NH)
                if s == 0:
                    dve.wait_ge(sig["du"], b.of(1, 1))
                if h == 0:
                    dve.wait_ge(sig["B_in"], b.of(NS, n + 1))
                since(dve, sig["y_sum"], b.of(STEPS, s - 3))
                V.tensor_tensor(st[:, s % 4], Bps[:], du[:, par, h], ALU.mult).then_inc(sig["dBu"], 1)

            def scan(s, b):
                dve.wait_ge(sig["dA"], b.of(STEPS, s + 1))
                dve.wait_ge(sig["dBu"], b.of(STEPS, s + 1))
                V.tensor_tensor_scan(st[:, s % 4], dA[:, s % 2], st[:, s % 4], 0.0, ALU.mult, ALU.add
                                     ).then_inc(sig["scan"], 1)

            def add_state(s, b, par):
                n, h = divmod(s, NH)
                dve.wait_ge(sig["P"], b.of(STEPS, s + 1))
                if n == 0:
                    V.scalar_tensor_tensor(y[:, h], u[:, par, h], W["dskip"][:, h:h + 1], st[:, s % 4],
                                           ALU.mult, ALU.add).then_inc(sig["y_sum"], 1)
                else:
                    dve.wait_ge(sig["y_sum"], b.of(STEPS, s - 1))
                    V.tensor_tensor(y[:, h], y[:, h], st[:, s % 4], ALU.add).then_inc(sig["y_sum"], 1)

            def c_step(step, b, par):
                if step[0] == "y":
                    for s in range(STEPS - SUM_LAG, STEPS):
                        add_state(s, b, par)
                    dve.wait_ge(sig["y_sum"], b.of(STEPS, STEPS))
                    V.tensor_tensor(du[:, par], y[:], zg[:, par], ALU.mult).then_inc(sig["yo"], 1)
                else:
                    filled(dve, "C", step, b)
                    since(dve, sig["out"], b.of(16))
                    V.tensor_tensor(ot[:], tiles(bank("C", step)[:]), xn1_tok[:, par], ALU.add
                                    ).then_inc(free["C"][BANK["C", step]], 1)
                    emptied(dve, "C", step, b)
                    dve.wait_ge(sig["g1"], b.of(1, 1))
                    V.scalar_tensor_tensor(ot[:], ot[:], 0.5, g1[:], ALU.mult, ALU.mult).then_inc(sig["s1"], 1)

            def do(g, step, it, par):
                if g == "A":
                    a_step(step, it + 1, 1 - par)
                elif g == "F":
                    f_step(step, it, par)
                else:
                    c_step(step, it + -1, 1 - par)

            def body(it, par, groups):
                lk["A"], lk["F"] = Link(dve, "dve", "A", it + 1), Link(dve, "dve", "F", it)
                if "F" in groups:
                    scan_input(0, it, par)
                    deal = slots(groups)
                    for s in range(STEPS):
                        if s + 1 < STEPS:
                            scan_input(s + 1, it, par)
                        scan(s, it)
                        if s >= SUM_LAG:
                            add_state(s - SUM_LAG, it, par)
                        for g, step in deal[s]:
                            do(g, step, it, par)
                else:
                    for g, step in ORDER:
                        if g in groups:
                            do(g, step, it, par)
                for g in "AF":
                    if g in groups:
                        lk[g].end()

            def prepare():
                dve.wait_ge(loads["ffn1"], 16 * len(LOADS["ffn1"]))
                dve.wait_ge(prep_pe, 1)
                V.tensor_tensor(b1f[:], facc["F"][:, 0:NCH["F"]], b1f[:], ALU.add)
                for e in range(E):
                    last = V.tensor_scalar(W["w1f"][:, e * H1:(e + 1) * H1], W["w1f"][:, e * H1:(e + 1) * H1],
                                           W["gammaT"][:, e:e + 1], None, ALU.mult)
                last.then_inc(prep_dve, 1)
                dve.wait_ge(prep_act, 1)
                V.tensor_scalar(Aneg[:], Aneg[:], -1.0, None, ALU.mult).then_inc(prep_dve, 1)

            V.memset(neghalf[:], -0.5)
            V.memset(eps[:], EPS)
            V.memset(grep[:], 0.0)
            V.memset(xpad[:], 0.0)
            dve.wait_ge(loads["small"], 16 * len(LOADS["small"]))
            V.tensor_copy(sel[:], W["rowsel"][:].unsqueeze(2).broadcast_to([96, 32, 128]))
            V.tensor_copy(ident_b[:], ident[:])
            V.tensor_scalar(mask_b[:], ident[:], -(2.0 ** 126), None, ALU.mult).then_inc(prep_dve, 1)
            dve.wait_ge(loads["mamba"], 16 * len(LOADS["mamba"]))
            V.tensor_scalar(W["conv_w"][:], W["conv_w"][:], 0.5, None, ALU.mult)
            V.tensor_scalar(W["conv_b"][:], W["conv_b"][:], 0.5, None, ALU.mult)
            V.tensor_scalar(W["winT"][:], W["winT"][:], W["norm_w"][:], None, ALU.mult).then_inc(prep_dve, 1)
            run(dve, body, prepare)

        @block.gpsimd
        def _(pool):
            G = nc.gpsimd
            lk = {}

            def a_step(step, b, par):
                g = "A"
                name, i = step
                if name in ("ln0", "ln1"):
                    k = name[2]
                    pool.wait_ge(sig["mean" + k], b.of(1, 1))
                    lk[g](G.tensor_tensor(ve[:], mv[:, :, 1], eps[:], ALU.add))
                    last = G.tensor_tensor(rstd[:], ve[:], neghalf[:], ALU.pow)
                    if name == "ln0":
                        last.then_inc(sig["rstd0"], 1)
                    else:
                        lk[g](last)
                        lk[g](G.tensor_tensor(q2[:], rstd[:], rstd[:], ALU.mult))
                        lk[g](G.tensor_tensor(q2[:], q2[:], mv[:, :, 1], ALU.mult))
                        lk[g](G.tensor_tensor(q2[:], q2[:], eps[:], ALU.add))
                        G.tensor_tensor(rstd2[:], q2[:], neghalf[:], ALU.pow).then_inc(sig["rstd1"], 1)
                elif name == "ft":
                    emptied(pool, g, step, b)
                    G.tensor_tensor(x_tok[:, par], x_in[:], tmp, ALU.add).then_inc(sig["x1"], 1)
                elif name == "dl" and i == NH - 1:
                    pool.wait_ge(sig["sp"], b.of(1, 1))
                    d = delta[:, par]
                    G.tensor_tensor(d, rl, cv, ALU.add)
                    pool.wait_ge(sig["e_kept"], b.of(1, 1))
                    lk[g](G.tensor_tensor(ez, ab, ez, ALU.subtract))
                    lk[g](G.tensor_tensor(d, d, ez, ALU.add))
                    G.tensor_tensor(du[:, par], d, u[:, par], ALU.mult).then_inc(sig["du"], 1)

            def f_step(step, b, par):
                g = "F"
                name, i = step
                if name == "h":
                    emptied(pool, g, step, b)
                    emptied(pool, g, ("gb", i // (NCH[g] // E)), b)
                    G.tensor_tensor(hid[g][:, i % 4], hid[g][:, i % 4], gbs[g][:, i // (NCH[g] // E) % 2], ALU.mult
                                    ).then_inc(sig["gatedF"], 1)

            def times_c(s, b):
                n, h = divmod(s, NH)
                if h == 0:
                    pool.wait_ge(sig["C_out"], b.of(NS, n + 1))
                pool.wait_ge(sig["scan"], b.of(STEPS, s + 1))
                G.tensor_tensor(st[:, s % 4], st[:, s % 4], Cs[:, n % 2], ALU.mult).then_inc(sig["P"], 1)

            def do(g, step, it, par):
                if g == "A":
                    a_step(step, it + 1, 1 - par)
                elif g == "F":
                    f_step(step, it, par)
                elif step[0] == "op":
                    b = it + -1
                    pool.wait_ge(sig["s1"], b.of(1, 1))
                    G.tensor_tensor(ot[:], ot[:], x_tok[:, 1 - par], ALU.add).then_inc(sig["ot"], 1)

            def body(it, par, groups):
                lk["A"] = Link(pool, "pool", "A", it + 1)
                if "F" in groups:
                    deal = slots(groups)
                    for s in range(STEPS):
                        times_c(s, it)
                        for g, step in deal[s]:
                            do(g, step, it, par)
                else:
                    for g, step in ORDER:
                        if g in groups:
                            do(g, step, it, par)
                if "A" in groups:
                    lk["A"].end()

            run(pool, body)


def layouts(i):
    def halves(a):
        return a.reshape(NH, 128, -1).transpose(1, 0, 2).reshape(128, -1)

    xp = i["L1_attn_x_proj_w"]
    bcrows = xp[RANK:]
    bc3 = np.concatenate([bcrows] * 3 + [xp[:RANK]], 0).T
    col = lambda a: a.reshape(-1, 128).T
    return {
        "x": i["L0_attn_x"],
        **CONSTS,
        "wqT": i["L0_attn_Wq"].T, "wkT": i["L0_attn_Wk"].T, "wvT": i["L0_attn_Wv"].T,
        "bq": col(i["L0_attn_bq"]), "bk": col(i["L0_attn_bk"]),
        "bv": np.broadcast_to(i["L0_attn_bv"], (128, D)),
        "gate": i["L0_ffn_gate"],
        "w1a": i["L0_ffn_W1"].transpose(1, 0, 2).reshape(D, -1),
        "b1a": col(i["L0_ffn_b1"]),
        "w2a": i["L0_ffn_W2"].reshape(-1, 128, D).transpose(1, 0, 2).reshape(128, -1),
        "b2a": i["L0_ffn_b2"],
        "norm_w": col(i["L1_attn_norm_w"]),
        "winT": i["L1_attn_in_proj_w"].T,
        "conv_w": halves(i["L1_attn_conv_w"]), "conv_b": col(i["L1_attn_conv_b"]),
        "xpBC": halves(bc3),
        "dtpT": i["L1_attn_dt_proj_w"].T, "dtb": col(i["L1_attn_dt_proj_b"]),
        "alog": halves(i["L1_attn_A_log"]), "dskip": col(i["L1_attn_D"]),
        "woutT": halves(i["L1_attn_out_proj_w"].T),
        "centT": i["L1_ffn_centroids"].T, "gammaT": i["L1_ffn_gamma"].T, "betaT": i["L1_ffn_beta"].T,
        "w1f": i["L1_ffn_W1"].transpose(2, 0, 1).reshape(D, -1),
        "b1f_raw": col(i["L1_ffn_b1"]),
        "w2f": i["L1_ffn_W2"].reshape(E, D, H1 // 128, 128).transpose(3, 0, 2, 1).reshape(128, -1),
        "b2f": i["L1_ffn_b2"],
    }


def kernel(**inputs):
    import concourse.bacc as _bacc
    from concourse.bass_utils import run_bass_kernel_spmd as _run

    nc = _bacc.Bacc("TRN2", target_bir_lowering=False, num_devices=1)
    arrays, ins = {}, {}
    for name, a in layouts({k: np.asarray(v) for k, v in inputs.items()}).items():
        a = np.ascontiguousarray(a)
        arrays[f"in_{name}_dram"] = a
        t = nc.dram_tensor(f"in_{name}_dram", a.shape, mybir.dt.from_np(a.dtype), kind="ExternalInput")
        ins[name] = (t.ap(), list(a.shape))
    out = nc.dram_tensor("out_dram", (NB, T, D), F32, kind="ExternalOutput").ap()
    build(nc, ins, out)
    r = _run(nc, [arrays], core_ids=[0])
    return r.results[0]["out_dram"]
```

```python
from contextlib import ExitStack

import numpy as np

import concourse.bass as bass
from concourse import mybir

F32 = mybir.dt.float32
BF16 = mybir.dt.bfloat16
I32, U32 = mybir.dt.int32, mybir.dt.uint32
ALU = mybir.AluOpType
ACT = mybir.ActivationFunctionType
AX = mybir.AxisListType

NB, T, D = 8, 512, 128
SUM_LAG = 2
NT = T // 128
E = 8
H0, H1 = 256, 512
NCH = E * H0 // 128
ST = (T - E) // 128 + E
NG = -(-ST // 4)
HC = H1 // 128
DI, NS, TAPS, RANK = 256, 16, 4, 8
NH = DI // 128
STEPS = NS * NH
EPS = 1e-5
PAIRED = 1 + (NB - 3) // 2 * 2
LAG = 3
BANKS = 4


def chunk_steps():
    out = []
    for c in range(NCH + LAG):
        if c < NCH:
            if c % (NCH // E) == 0:
                out.append(("gb", c // (NCH // E)))
            out.append(("h", c))
        if c >= LAG:
            out.append(("m", c - LAG))
    return out


def tile_steps():
    out = [("xs", 0), ("ld", 1)]
    for j in range(ST + 2):
        if j < ST:
            out.append(("h", j))
        if j % 4 == 1 and j // 4 + 1 < NG:
            k = j // 4 + 1
            out.append(("xs", k))
            if k + 1 < NG:
                out.append(("ld", k + 1))
        if 1 <= j <= ST:
            out.append(("t", j - 1))
        if j >= 2:
            out.append(("y", j - 2))
            if (j - 2) % 4 == 3 or j - 2 == ST - 1:
                out += [("ye", (j - 2) // 4), ("st", (j - 2) // 4)]
    return out


def at(group, start, end, steps):
    return [(start + (end - start) * k / len(steps), group, s) for k, s in enumerate(steps)]


def each(name, n):
    return [(name, i) for i in range(n)]


PLACES = (
    at("C", 0.0000, 0.0040, [("xr", 0)]) + at("C", 0.0000, 0.0040, [("y", 0)]) + at("C", 0.0459, 0.0499, [("op", 0)])
    + at("A", 0.0000, 0.0100, [("xin", 0)]) + at("A", 0.0300, 0.0400, [("ln0", 0)]) + at("A", 0.0600, 0.0700, [("xT", 0)])
    + at("A", 0.0700, 0.1100, [("gl", 0), ("q", 0), ("k", 0), ("v", 0)])
    + at("A", 0.0889, 0.1016, [("gate", 0)]) + at("A", 0.1147, 0.1894, each("s", NT)) + at("A", 0.1530, 0.1580, [("gT", 0)])
    + at("A", 0.1953, 0.1993, [("b2", 0)]) + at("A", 0.1980, 0.2480, each("p", NT)) + at("A", 0.2783, 0.2883, [("o", 0)])
    + at("A", 0.2180, 0.8074, chunk_steps())
    + at("A", 0.8551, 0.8591, [("silu", 0)]) + at("A", 0.9351, 0.9451, [("ft", 0)])
    + at("H", 0.0400, 0.0500, [("keep", 0)]) + at("H", 0.3100, 0.3200, [("ln1", 0)])
    + at("H", 0.3700, 0.3904, [("x1T", 0), ("hT", 0)]) + at("H", 0.4304, 0.5204, each("xi", NH) + each("z", NH))
    + at("H", 0.5610, 0.5710, [("sc", 0)]) + at("H", 0.6275, 0.6375, [("bc", 0)]) + at("H", 0.6583, 0.6983, each("dl", NH))
    + at("H", 0.7259, 0.7359, [("rk", 0)]) + at("H", 0.7424, 0.7524, [("ln", 0)]) + at("H", 0.7883, 0.8483, each("du", NH))
    + at("H", 0.7583, 0.8183, each("put", NT))
    + at("H", 0.8983, 0.9083, [("fetch", 0)])
    + at("F", 0.0150, 0.8000, tile_steps())
    + at("F", 0.8600, 0.9142, each("get", NT)) + at("F", 0.9676, 0.9716, [("ft", 0)]) + at("F", 0.9850, 0.9890, [("silu", 0)]))
PLACES.sort(key=lambda x: x[0])
ORDER = [(g, s) for _, g, s in PLACES]
assert ORDER.index(("A", ("gT", 0))) < ORDER.index(("A", ("s", NT - 1)))
NO_BANK = {("A", k) for k in ("xin", "ln0", "gate", "b2", "m", "silu")} | {
    ("H", k) for k in ("keep", "fetch", "ln1", "ln", "du", "put")} | {("C", "xr"), ("C", "y")} | {
    ("F", k) for k in ("ld", "y", "ye", "st", "get", "ft", "silu")}
AHEAD = {"A": 2, "H": 1, "F": 0, "C": -1}


def groups_of(it):
    return "".join(g for g in "AHFC" if 0 <= it + AHEAD[g] < NB)


def slots(groups):
    return [[(g, s) for t, g, s in PLACES if g in groups and int(t * STEPS) == k] for k in range(STEPS)]


JOBS = {g: [s for gg, s in ORDER if gg == g and (g, s[0]) not in NO_BANK] for g in "AHFC"}
BANK = {}
for _g, _s in ORDER:
    if (_g, _s[0]) not in NO_BANK:
        BANK[_g, _s] = len(BANK) % BANKS
IN_BANK = {g: [[s for s in JOBS[g] if BANK[g, s] == k] for k in range(BANKS)] for g in "AHFC"}
LINKS = {("dve", "A"): 32, ("dve", "H"): 48, ("pool", "A"): 2, ("pool", "H"): 8}


class Batch:

    def __init__(self, eng, reg, plus, products=None):
        self.eng, self.reg, self.plus = eng, reg, plus
        self.products = {1: reg} if products is None else products

    def __add__(self, n):
        return Batch(self.eng, self.reg, self.plus + n, self.products)

    def of(self, k, more=0):
        if self.reg is None:
            return self.plus * k + more
        if k not in self.products:
            self.products[k] = self.eng.snap(self.reg * k)
        return self.products[k] + (self.plus * k + more)

    def is_(self, n):
        return self.reg is None and self.plus == n

CONSTS = {
    "ident": np.eye(128, dtype=np.float32),
    "rowsel": np.tile(np.eye(32, dtype=np.float32), (3, 1)),
    "before": np.triu(np.ones((128, 128), np.float32), 1),
    "full": np.tile(np.arange(4, dtype=np.float32) * 128, (128, 1)),
    "tile_no": np.arange(ST, dtype=np.float32)[None],
    "first": np.tile(np.arange(E, 0, -1, dtype=np.float32), (128, NT, 1)).reshape(128, NT * E),
}


def build(nc, ins, out, xs_dram, ys_dram, kept_dram):
    nc.disable_value_cache = True
    ctx = ExitStack()
    with ctx:
        def sb(name, shape, dt=F32):
            return ctx.enter_context(nc.sbuf_tensor(name, shape, dt))

        def sem(name):
            return ctx.enter_context(nc.semaphore(name))

        hs = sb("hs", [128, 2, H1])
        hsT = sb("hsT", [128, 2, H1])
        W = {"b1r": hs[0:96, 0], "b2r": hs[0:96, 1, 0:D], "before": hs[:, 1, D:D + 128]}
        betaM = hsT[:].rearrange("p a b -> p (a b)")[:, 0:E * 96]
        for name, (_, shape) in ins.items():
            if name != "x" and name not in W:
                W[name] = sb("w_" + name, [128, shape[1]] if name == "dtpT" else shape)
        sel = sb("sel", [96, 32, 128], BF16)
        ident_b = sb("ident_b", [128, 128], BF16)
        mask_b = sb("mask_b", [128, 128], BF16)
        neghalf = sb("neghalf", [128, NT])
        eps = sb("eps", [128, NT])
        bqs = sb("bqs", [128, 1])
        Aneg = sb("Aneg", [128, NH * NS])
        ident = W["ident"]
        b1p = sb("b1p", [96, H1], BF16)
        b2p = sb("b2p", [96, D], BF16)
        before_b = sb("before_b", [128, 128], BF16)
        ones_b = sb("ones_b", [128, 128], BF16)

        x_in = sb("x_in", [128, NT, D])
        x_tok = sb("x_tok", [128, NT, D])
        xr = sb("xr", [128, NT, D])
        ot = sb("ot", [128, NT, D])
        stats = sb("stats", [128, NT, 6])
        mv = sb("mv", [128, NT, 2])
        ve = sb("ve", [128, NT])
        rstd = sb("rstd", [128, NT])
        xnT = sb("xnT", [128, T])
        qkv = sb("qkv", [128, 5, T])
        qT, kT = qkv[:, 0], qkv[:, 1]
        v_tok, xn_tok = (qkv[:, k].rearrange("p (i d) -> p i d", i=NT) for k in (2, 3))
        s_tok = ot[:]
        hT = qkv[:, 1]
        ab, rl = qkv[:, 0:NH], qkv[:, NH:2 * NH]
        nmax = sb("nmax", [128, NT])
        rsum = sb("rsum", [128, NT])
        rs = sb("rs", [128, NT])
        prob = sb("prob", [128, NT, T])
        ht_tok = prob[:, 2].rearrange("p (i d) -> p i d", i=NT)
        rest = prob[0:96, 3]
        cv, ec = prob[:, 0:NH], prob[:, NH:2 * NH]
        probT = sb("probT", [128, NT, T])
        zr, ez = probT[:, 0:NH], probT[:, NH:2 * NH]
        gm = sb("gm", [128, NT])
        gr = sb("gr", [128, NT])
        gt = sb("gt", [128, NT, E])
        gp = sb("gp", [128, NT, E])
        eq = sb("eq", [128, NT, E])
        oh1 = sb("oh1", [128, NT, E])
        oh2 = sb("oh2", [128, NT, E])
        grep = sb("grep", [128, NT, 96])
        gTf = sb("gTf", [E, T])
        g3 = sb("g3", [96, T], BF16)
        midp = sb("midp", [96, T], BF16)
        gbs = sb("gbs", [128, 2, T])
        hid = sb("hid", [128, 4, T])
        se, g0T = hid[:, 0], hid[:, 1]
        tmp = hid[:, 2].rearrange("p (i d) -> p i d", i=NT)
        q2 = sb("q2", [128, NT])
        rstd2 = sb("rstd2", [128, NT])
        xn1_tok = sb("xn1_tok", [128, 2, NT, D])
        xn1T = sb("xn1T", [128, T])
        xpad = qkv[:, 2:5].rearrange("p a b -> p (a b)")[:, 0:NH * (TAPS - 1 + T)].rearrange("p (h c) -> p h c", h=NH)
        u = sb("u", [128, 2, NH, T])
        zg = sb("zg", [128, 2, NH, T])
        bc3 = sb("bc3", [96, 2, T], BF16)
        dt8 = sb("dt8", [128, T])
        delta = sb("delta", [128, 2, NH, T])
        du = sb("du", [128, 2, NH, T])
        am = sb("am", [128, NT])
        alpha = sb("alpha", [128, 2, NT])
        ohr = sb("ohr", [128, NT, E])
        ohb = sb("ohb", [128, NT, E], BF16)
        more = sb("more", [128, E, 4])
        ntile = sb("ntile", [128, E])
        endt = sb("endt", [128, E])
        ones8 = sb("ones8", [128, E])
        posr = sb("posr", [128, NT, E])
        posf = sb("posf", [128, NT])
        pos = sb("pos", [128, 2, NT], U32)
        upto = sb("upto", [1, ST, E])
        texf = sb("texf", [1, ST])
        texp = sb("texp", [1, 2, ST], I32)
        xs_in = sb("xs_in", [128, 4, D])
        xsT = sb("xsT", [128, 2, T])
        ys = sb("ys", [128, 4, D])
        fe = sb("fe", [128, NT, D])
        g1 = ys
        dA = sb("dA", [128, 2, T])
        st = sb("st", [128, 4, T])
        Bs = sb("Bs", [128, 2, T])
        Cs = sb("Cs", [128, 2, T])
        y = sb("y", [128, NH, T])

        work = [ctx.enter_context(nc.psum_tensor(f"work{k}", [128, T], F32)) for k in range(BANKS)]
        facc = ctx.enter_context(nc.psum_tensor("facc", [128, T], F32))
        yps = ctx.enter_context(nc.psum_tensor("yps", [128, T], F32))
        Bps = ctx.enter_context(nc.psum_tensor("Bps", [128, T], F32))
        Cps = ctx.enter_context(nc.psum_tensor("Cps", [128, T], F32))

        loads = {k: sem("load_" + k) for k in ("small", "ffn0", "mamba", "ffn1")}
        ready = {g: sem("ready" + g) for g in "AHFC"}
        free = {g: [sem(f"free{g}{k}") for k in range(BANKS)] for g in "AHFC"}
        chain = {k: sem("chain_%s_%s" % k) for k in LINKS}
        prep_act, prep_pe, prep_dve, prep_own, prep_memset = (sem("prep_" + k) for k in ("act", "pe", "dve", "own", "memset"))
        sig = {n: sem(n) for n in (
            "x_in", "stats", "mean0", "rstd0", "xn0", "smax", "g_in", "g_exp", "g_rep", "g_hi", "g_split", "hot",
            "siluA_e", "g0T", "x1", "mean1", "rstd1", "xn1", "ht", "cv", "pos", "put", "go", "sp_go", "kept", "xr", "xs_ld", "xs_zero", "ye", "ys_out", "got", "ec", "u", "zg", "bc_hi", "bc3",
            "e_out", "sp", "e_kept", "du0", "du1", "gated_dve", "gated_pool", "usedA", "usedF", "a_exp", "alpha", "r1", "siluF_e",
            "g1", "B_in", "C_in", "B_out", "C_out", "dA", "dBu0", "dBu1", "scan", "P", "y_sum", "yo", "s1", "ot", "out")}

        def since(eng, semaphore, value):
            if not isinstance(value, int) or value > 0:
                eng.wait_ge(semaphore, value)

        def filled(eng, g, step, b):
            eng.wait_ge(ready[g], b.of(len(JOBS[g]), JOBS[g].index(step) + 1))

        def emptied(eng, g, step, b):
            k = BANK[g, step]
            eng.wait_ge(free[g][k], b.of(len(IN_BANK[g][k]), IN_BANK[g][k].index(step) + 1))

        def bank_free(eng, g, step, it, groups):
            k = BANK[g, step]

            def jobs_of(present):
                return [(gg, s) for gg, s in ORDER if gg in present and BANK.get((gg, s)) == k]

            run = jobs_of(groups)
            at = run.index((g, step))
            if at:
                gg, s = run[at - 1]
                emptied(eng, gg, s, it + AHEAD[gg])
            else:
                before = jobs_of(groups_of(it.plus - 1) if it.reg is None else "AHF")
                if before:
                    gg, s = before[-1]
                    emptied(eng, gg, s, it + (AHEAD[gg] - 1))

        gated = (sig["gated_dve"], sig["gated_pool"])

        def gate_hidden(eng, vector, i, b):
            emptied(eng, "A", ("h", i), b)
            emptied(eng, "A", ("gb", i // (NCH // E)), b)
            vector.tensor_tensor(hid[:, i % 4], hid[:, i % 4], gbs[:, i // (NCH // E) % 2], ALU.mult
                                 ).then_inc(gated[i % 2], 1)

        def finish_delta(eng, vector, link, h, b, par):
            eng.wait_ge(sig["e_kept"], b.of(NH, h + 1))
            eng.wait_ge(sig["sp"], b.of(NH, h + 1))
            link(vector.tensor_tensor(delta[:, par, h], rl[:, h], cv[:, h], ALU.add))
            vector.tensor_tensor(du[:, par, h], delta[:, par, h], u[:, par, h], ALU.mult).then_inc(sig["du%d" % h], 1)

        dBu = (sig["dBu0"], sig["dBu1"])

        def scan_input(eng, vector, s, b, par):
            n, h = divmod(s, NH)
            if n == 0:
                eng.wait_ge(sig["du%d" % h], b.of(1, 1))
            eng.wait_ge(sig["B_out"], b.of(NS, n + 1))
            since(eng, sig["y_sum"], b.of(STEPS, s - 3))
            vector.tensor_tensor(st[:, s % 4], Bs[:, n % 2], du[:, par, h], ALU.mult).then_inc(dBu[h], 1)

        def bank(g, step):
            return work[BANK[g, step]]

        def tiles(ap):
            return ap.rearrange("p (i d) -> p i d", i=NT)

        class Link:

            def __init__(self, eng, who, g, b):
                self.eng, self.key, self.b, self.n = eng, (who, g), b, 0

            def __call__(self, ins):
                self.n += 1
                assert self.n <= LINKS[self.key], self.key
                ins.then_inc(chain[self.key], 1)
                self.eng.wait_ge(chain[self.key], self.b.of(LINKS[self.key], self.n))

            def end(self):
                if self.n < LINKS[self.key]:
                    self.eng.sem_inc(chain[self.key], LINKS[self.key] - self.n)

        def run(eng, body, after_first=None, before_scan=None):
            const = Batch(eng, None, 0)
            for it in range(-2, 1):
                body(const + it, it % 2, groups_of(it))
                if it == -2 and after_first:
                    after_first()
                if it == -1 and before_scan:
                    before_scan()
            with eng.Fori(1, PAIRED, 2) as reg:
                it = Batch(eng, reg, 0)
                body(it, 1, "AHFC")
                body(it + 1, 0, "AHFC")
            for it in range(PAIRED, NB + 1):
                body(const + it, it % 2, groups_of(it))

        block = ctx.enter_context(nc.Block())

        LOADS = {"small": ["ident", "rowsel", "first", "before", "full", "tile_no", "wqT", "wkT", "wvT", "bq", "bk", "bv", "gate"],
                 "ffn0": ["w1a", "b1a", "w2a", "b2a"],
                 "mamba": ["norm_w", "winT", "conv_w", "conv_b", "xpBC", "dtpT", "dtb", "alog", "dskip",
                           "woutT"],
                 "ffn1": ["centT", "gammaT", "betaT", "w1f", "b1r", "w2f", "b2r"]}

        @block.sync
        def _(sp):
            def load_x(b):
                n = b.of(1)
                if b.reg is not None:
                    n = nc.s_assert_within(n, 3, NB - 1, skip_runtime_bounds_check_because="the loop ends before the last batch")
                sp.dma_start(x_in[:], ins["x"][0][n].rearrange("(i p) d -> p i d", p=128)
                             ).then_inc(sig["x_in"], 16)

            def body(it, par, groups):
                for k in (NG, 16, 16 * NG, 16 * NT, len(JOBS["F"])):
                    it.of(k)
                for g, step in ORDER:
                    name, k = step
                    if g == "F" and g in groups:
                        b = it
                        tiles_k = min(4, ST - 4 * k)
                        if name == "ld":
                            filled(sp, g, ("xs", k - 1), b)
                            sp.dma_start(xs_in[:, 0:tiles_k], xs_dram[4 * k:4 * k + tiles_k].rearrange("i p d -> p i d")
                                         ).then_inc(sig["xs_ld"], 16)
                        elif name == "st":
                            if k == 0:
                                since(sp, sig["got"], b.of(16 * NT))
                                sp.sem_inc(sig["sp_go"], 1)
                            sp.wait_ge(sig["ye"], b.of(NG, k + 1))
                            sp.dma_start(ys_dram[4 * k:4 * k + tiles_k].rearrange("i p d -> p i d"), ys[:, 0:tiles_k]
                                         ).then_inc(sig["ys_out"], 16)
                    elif g == "A" and g in groups and name == "xin" and not it.is_(-2):
                        b = it + 2
                        sp.wait_ge(sig["x1"], b.of(1))
                        sp.sem_inc(sig["sp_go"], 1)
                        load_x(b)
                    elif g == "H" and g in groups and name == "fetch":
                        b = it + 1
                        if "F" in groups:
                            filled(sp, "F", ("xs", NG - 1), it)
                            sp.sem_inc(sig["sp_go"], 1)
                        sp.wait_ge(sig["put"], b.of(16 * NT, 16 * NT))
                        sp.dma_start(xs_in[:], xs_dram[0:4].rearrange("i p d -> p i d")).then_inc(sig["xs_ld"], 16)
                    elif g == "H" and g in groups and name == "keep":
                        b = it + 1
                        since(sp, sig["xr"], b.of(16, -16))
                        sp.sem_inc(sig["sp_go"], 1)
                        sp.wait_ge(sig["x1"], b.of(1, 1))
                        sp.dma_start(kept_dram[1 - par].rearrange("(i p) d -> p i d", p=128), x_tok[:]
                                     ).then_inc(sig["kept"], 16)
                    elif g == "C" and g in groups and name == "xr":
                        b = it + -1
                        since(sp, sig["ot"], b.of(1))
                        sp.sem_inc(sig["sp_go"], 1)
                        sp.wait_ge(sig["kept"], b.of(16, 16))
                        sp.dma_start(xr[:], kept_dram[1 - par].rearrange("(i p) d -> p i d", p=128)
                                     ).then_inc(sig["xr"], 16)
                    elif g == "C" and g in groups and name == "op":
                        b = it + -1
                        sp.wait_ge(sig["ot"], b.of(1, 1))
                        sp.dma_start(out[b.of(1)].rearrange("(i p) d -> p i d", p=128), ot[:]).then_inc(sig["out"], 16)

            load_x(Batch(sp, None, 0))
            for part, names in LOADS.items():
                for name in names:
                    sp.dma_start(W[name][96:96 + RANK] if name == "dtpT" else W[name][:], ins[name][0]).then_inc(loads[part], 16)
            sp.wait_ge(prep_dve, 1)
            for k in range(NG):
                n = min(4, ST - 4 * k)
                sp.dma_start(xs_dram[4 * k:4 * k + n].rearrange("i p d -> p i d"), fe[:, 0:n]).then_inc(sig["xs_zero"], 16)
            run(sp, body)
            sp.wait_ge(sig["out"], 16 * NB)

        @block.tensor
        def _(pe):
            mm = nc.tensor.matmul
            pe.wait_ge(loads["small"], 16 * len(LOADS["small"]))
            pe.wait_ge(prep_dve, 1)

            def a_step(g, step, it, par, groups):
                b = it + AHEAD[g]
                name, i = step
                if (g, name) not in NO_BANK:
                    bank_free(pe, g, step, it, groups)
                    w = bank(g, step)
                last = None
                if name == "xT":
                    pe.wait_ge(sig["xn0"], b.of(1, 1))
                    for t in range(NT):
                        last = nc.tensor.transpose(w[:, t * 128:(t + 1) * 128], xn_tok[:, t], ident[:])
                elif name == "gl":
                    emptied(pe, g, ("xT", 0), b)
                    for t in range(NT):
                        last = mm(w[:, t * E:(t + 1) * E], xnT[:, t * 128:(t + 1) * 128], W["gate"][:],
                                  start=True, stop=True)
                elif name in ("q", "k"):
                    last = mm(w[:], W["wqT" if name == "q" else "wkT"][:], xnT[:], start=True, stop=True)
                elif name == "v":
                    for t in range(NT):
                        last = mm(w[:, t * 128:(t + 1) * 128], xnT[:, t * 128:(t + 1) * 128], W["wvT"][:],
                                  start=True, stop=True)
                elif name == "s":
                    if i == 0:
                        emptied(pe, g, ("q", 0), b)
                        emptied(pe, g, ("k", 0), b)
                    mm(w[:], qT[:, i * 128:(i + 1) * 128], kT, start=True, stop=False)
                    last = mm(w[:, i * 128:(i + 1) * 128], ident_b[:], mask_b[:], start=False, stop=True)
                elif name == "p":
                    if i == 0:
                        for t in range(NT):
                            emptied(pe, g, ("s", t), b)
                    for t in range(NT):
                        last = nc.tensor.transpose(w[:, t * 128:(t + 1) * 128], prob[:, t, i * 128:(i + 1) * 128],
                                                   ident[:])
                elif name == "o":
                    emptied(pe, g, ("v", 0), b)
                    for m in range(NT):
                        emptied(pe, g, ("p", m), b)
                    for t in range(NT):
                        for m in range(NT):
                            last = mm(w[:, t * 128:(t + 1) * 128], probT[:, m, t * 128:(t + 1) * 128], v_tok[:, m],
                                      start=(m == 0), stop=(m == NT - 1))
                elif name == "gT":
                    pe.wait_ge(sig["g_rep"], b.of(1, 1))
                    for t in range(NT):
                        last = nc.tensor.transpose(w[0:96, t * 128:(t + 1) * 128], grep[:, t], ident[:])
                elif name == "ft":
                    pe.wait_ge(sig["g0T"], b.of(1, 1))
                    for t in range(NT):
                        last = nc.tensor.transpose(w[:, t * 128:(t + 1) * 128], g0T[:, t * 128:(t + 1) * 128], ident[:])
                elif name == "x1T":
                    pe.wait_ge(sig["xn1"], b.of(1, 1))
                    for t in range(NT):
                        last = nc.tensor.transpose(w[:, t * 128:(t + 1) * 128], xn1_tok[:, par, t], ident[:])
                elif name == "hT":
                    pe.wait_ge(sig["ht"], b.of(1, 1))
                    for t in range(NT):
                        last = nc.tensor.transpose(w[:, t * 128:(t + 1) * 128], ht_tok[:, t], ident[:])
                elif name in ("xi", "z"):
                    if step == ("xi", 0):
                        emptied(pe, g, ("hT", 0), b)
                        if b.is_(0):
                            pe.wait_ge(loads["mamba"], 16 * len(LOADS["mamba"]))
                            pe.wait_ge(prep_dve, 2)
                    c = i + (NH if name == "z" else 0)
                    last = mm(w[:], W["winT"][:, c * 128:(c + 1) * 128], hT, start=True, stop=True)
                elif name == "sc":
                    emptied(pe, g, ("x1T", 0), b)
                    if b.is_(0):
                        pe.wait_ge(loads["ffn1"], 16 * len(LOADS["ffn1"]))
                    for t in range(NT):
                        last = mm(w[:, t * E:(t + 1) * E], xn1T[:, t * 128:(t + 1) * 128], W["centT"][:],
                                  start=True, stop=True)
                elif name == "rk":
                    pe.wait_ge(sig["hot"], b.of(1, 1))
                    for t in range(NT):
                        r = w[:, t * E:(t + 1) * E]
                        mm(r, before_b[:], ohb[:, t], start=True, stop=(t == 0))
                        for m in range(t):
                            mm(r, ones_b[:], ohb[:, m], start=False, stop=(m == t - 1))
                    for m in range(NT):
                        last = mm(w[:, NT * E:(NT + 1) * E], ones_b[:], ohb[:, m], start=(m == 0), stop=(m == NT - 1))
                elif name == "bc":
                    pe.wait_ge(sig["u"], b.of(NH, NH))
                    rows = 96 + RANK
                    for h in range(NH):
                        last = mm(w[0:rows], W["xpBC"][:, h * rows:(h + 1) * rows], u[:, par, h],
                                  start=(h == 0), stop=(h == NH - 1))
                elif name == "dl":
                    emptied(pe, g, ("bc", 0), b)
                    last = mm(w[:], W["dtpT"][96:96 + RANK, i * 128:(i + 1) * 128], dt8[96:96 + RANK],
                              start=True, stop=True)
                else:
                    last = expert_step(step, b)
                if last is not None and (g, name) not in NO_BANK:
                    last.then_inc(ready[g], 1)

            def expert_step(step, b):
                g = "A"
                name, i = step
                if name == "b2":
                    emptied(pe, g, ("gT", 0), b)
                    since(pe, sig["g0T"], b.of(1))
                    if b.is_(0):
                        pe.wait_ge(loads["ffn0"], 16 * len(LOADS["ffn0"]))
                    return mm(facc[:], W["b2a"][:], gTf[:], start=True, stop=False)
                if name == "gb":
                    if i == 0:
                        pe.wait_ge(sig["g_split"], b.of(1, 1))
                    return mm(bank(g, step)[:], sel[:, i], g3[:], start=True, stop=True)
                if name == "h":
                    return mm(bank(g, step)[:], W["w1a"][:, i * 128:(i + 1) * 128], xnT[:], start=True, stop=True)
                if name == "m":
                    pe.wait_ge(gated[i % 2], b.of(NCH // 2, i // 2 + 1))
                    return mm(facc[:], W["w2a"][:, i * 128:(i + 1) * 128], hid[:, i % 4],
                              start=False, stop=(i == NCH - 1)).then_inc(sig["usedA"], 1)

            f_par = [0]
            expert_of = {}

            def f_step(step, it, par, groups):
                b = it
                g = "F"
                name, i = step
                f_par[0] = par
                if name == "h":
                    e = expert_of[i] = pe.value_load(texp[0:1, par, i:i + 1], min_val=0, max_val=E - 1)
                if (g, name) not in NO_BANK:
                    bank_free(pe, g, step, it, groups)
                    w = bank(g, step)
                if name == "xs":
                    if i == 0:
                        pe.wait_ge(sig["pos"], b.of(1, 1))
                    pe.wait_ge(sig["xs_ld"], b.of(16 * NG, 16 * (i + 1)))
                    for t in range(min(4, ST - 4 * i)):
                        last = nc.tensor.transpose(w[:, t * 128:(t + 1) * 128], xs_in[:, t], ident[:])
                    last.then_inc(ready[g], 1)
                elif name == "h":
                    if i % 4 == 0:
                        emptied(pe, g, ("xs", i // 4), b)
                    mm(w[:], sel[:, bass.ds(e, 1)].rearrange("p a b -> p (a b)"), b1p[:], start=True, stop=False)
                    mm(w[:], xsT[:, i // 4 % 2, i % 4 * 128:(i % 4 + 1) * 128], W["w1f"][:, bass.ds(e * H1, H1)],
                       start=False, stop=True).then_inc(ready[g], 1)
                elif name == "t":
                    emptied(pe, g, ("h", i), b)
                    for c in range(HC):
                        last = nc.tensor.transpose(w[:, c * 128:(c + 1) * 128], hs[:, i % 2, c * 128:(c + 1) * 128], ident[:])
                    last.then_inc(ready[g], 1)
                elif name == "y":
                    emptied(pe, g, ("t", i), b)
                    if i % 4 == 0:
                        since(pe, sig["ye"], b.of(NG, i // 4))
                    e = expert_of[i]
                    r = yps[:, i % 4 * 128:(i % 4 + 1) * 128]
                    mm(r, sel[:, bass.ds(e, 1)].rearrange("p a b -> p (a b)"), b2p[:], start=True, stop=False)
                    for c in range(HC):
                        last = mm(r, hsT[:, i % 2, c * 128:(c + 1) * 128], W["w2f"][:, bass.ds(e * H1 + c * 128, 128)],
                                  start=False, stop=(c == HC - 1))
                    last.then_inc(sig["usedF"], 1)

            def spread(n, b, par):
                if n == 0:
                    pe.wait_ge(sig["bc3"], b.of(1, 1))
                since(pe, sig["B_out"], b.of(NS, n))
                mm(Bps[:], sel[:, n], bc3[:, par], start=True, stop=True).then_inc(sig["B_in"], 1)
                since(pe, sig["C_out"], b.of(NS, n))
                mm(Cps[:], sel[:, NS + n], bc3[:, par], start=True, stop=True).then_inc(sig["C_in"], 1)

            def project(it, groups):
                b, par = it + -1, 1 - f_par[0]
                bank_free(pe, "C", ("op", 0), it, groups)
                pe.wait_ge(sig["yo"], b.of(1, 1))
                for t in range(NT):
                    for h in range(NH):
                        last = mm(bank("C", ("op", 0))[:, t * 128:(t + 1) * 128], du[:, par, h, t * 128:(t + 1) * 128],
                                  W["woutT"][:, h * 128:(h + 1) * 128], start=(h == 0), stop=(h == NH - 1))
                last.then_inc(ready["C"], 1)

            def do(g, step, it, par, groups):
                if g in "AH":
                    a_step(g, step, it, 1 - par, groups)
                elif g == "F":
                    f_step(step, it, par, groups)
                elif step[0] == "op":
                    project(it, groups)

            def body(it, par, groups):
                f_par[0] = par
                if "F" not in groups:
                    for g, step in ORDER:
                        if g in groups:
                            do(g, step, it, par, groups)
                    return
                if it.is_(0):
                    spread(0, it, par)
                deal = slots(groups)
                for s in range(STEPS):
                    for g, step in deal[s]:
                        do(g, step, it, par, groups)
                    if s % NH == 0 and s // NH + 1 < NS:
                        spread(s // NH + 1, it, par)
                    elif s == STEPS - NH and "H" in groups:
                        spread(0, it + 1, 1 - par)

            def beta_products():
                pe.wait_ge(loads["ffn1"], 16 * len(LOADS["ffn1"]))
                pe.wait_ge(prep_dve, 3)
                for e in range(E):
                    last = mm(yps[0:96], betaM[:, e * 96:(e + 1) * 96], W["w1f"][:, e * H1:(e + 1) * H1],
                              start=(e == 0), stop=(e == E - 1))
                last.then_inc(prep_pe, 1)

            def weights_wait():
                pe.wait_ge(prep_dve, 4)

            run(pe, body, beta_products, weights_wait)

        @block.scalar
        def _(act):
            def go(out, in_, func, **k):
                return nc.scalar.activation(out, in_, func, **k)

            def expert_step(step, b):
                g = "A"
                name, i = step
                per = NCH // E
                filled(act, g, step, b)
                if name == "gb":
                    for s in gated:
                        since(act, s, b.of(NCH // 2, (i - 1) * per // 2 if i >= 2 else 0))
                    go(gbs[:, i % 2], bank(g, step)[:], ACT.Copy).then_inc(free[g][BANK[g, step]], 1)
                else:
                    since(act, sig["usedA"], b.of(NCH, i - 3 if i >= 4 else 0))
                    go(hid[:, i % 4], bank(g, step)[:], ACT.Relu, bias=W["b1a"][:, i:i + 1]
                       ).then_inc(free[g][BANK[g, step]], 1)

            def a_step(g, step, b, par):
                name, i = step
                fr = free[g][BANK[g, step]] if (g, name) not in NO_BANK else None
                w = bank(g, step) if (g, name) not in NO_BANK else None
                if name in ("gb", "h"):
                    expert_step(step, b)
                elif name == "xT":
                    filled(act, g, step, b)
                    since(act, sig["usedA"], b.of(NCH))
                    go(xnT[:], w[:], ACT.Copy).then_inc(fr, 1)
                elif name == "gl":
                    act.wait_ge(sig["g_in"], b.of(1, 1))
                    go(gp[:], gt[:], ACT.Exp).then_inc(sig["g_exp"], 1)
                elif name == "q":
                    filled(act, g, step, b)
                    go(qT, w[:], ACT.Identity, bias=bqs[:], scale=1.0 / D).then_inc(fr, 1)
                elif name == "k":
                    filled(act, g, step, b)
                    go(kT, w[:], ACT.Identity, bias=W["bk"][:]).then_inc(fr, 1)
                elif name == "s":
                    act.wait_ge(sig["smax"], b.of(NT, i + 1))
                    go(prob[:, i], w[:], ACT.Exp, bias=nmax[:, i:i + 1], accum_out=rsum[:, i:i + 1]).then_inc(fr, 1)
                elif name == "p":
                    filled(act, g, step, b)
                    go(probT[:, i], w[:], ACT.Copy).then_inc(fr, 1)
                elif name == "gT":
                    filled(act, g, step, b)
                    go(gTf[:], w[0:E], ACT.Copy)
                    go(g3[:], w[0:96], ACT.Copy).then_inc(sig["g_hi"], 1)
                elif name == "silu":
                    act.wait_ge(sig["usedA"], b.of(NCH, NCH))
                    go(se, facc[:], ACT.Tanh, scale=0.5).then_inc(sig["siluA_e"], 1)
                elif name == "x1T":
                    filled(act, g, step, b)
                    go(xn1T[:], w[:], ACT.Copy).then_inc(fr, 1)
                elif name == "hT":
                    filled(act, g, step, b)
                    go(hT, w[:], ACT.Copy).then_inc(fr, 1)
                elif name == "xi":
                    filled(act, g, step, b)
                    go(xpad[:, i, TAPS - 1:], w[:], ACT.Copy).then_inc(fr, 1)
                elif name == "z":
                    filled(act, g, step, b)
                    go(zr[:, i], w[:], ACT.Copy, scale=0.5)
                    go(ez[:, i], w[:], ACT.Tanh, scale=0.5).then_inc(fr, 1)
                    act.wait_ge(sig["cv"], b.of(NH, i + 1))
                    go(ec[:, i], cv[:, i], ACT.Tanh).then_inc(sig["ec"], 1)
                elif name == "bc":
                    filled(act, g, step, b)
                    go(dt8[96:96 + RANK], w[96:96 + RANK], ACT.Copy)
                    go(bc3[:, par], w[0:96], ACT.Copy).then_inc(sig["bc_hi"], 1)
                elif name == "sc":
                    act.wait_ge(sig["hot"], b.of(1, 1))
                    go(alpha[:, par], am[:], ACT.Exp, scale=-1.0).then_inc(sig["a_exp"], 1)
                elif name == "dl":
                    filled(act, g, step, b)
                    go(rl[:, i], w[:], ACT.Relu, bias=W["dtb"][:, i:i + 1])
                    go(ab[:, i], w[:], ACT.Abs, bias=W["dtb"][:, i:i + 1]).then_inc(fr, 1)
                    emptied(act, g, step, b)
                    go(ab[:, i], ab[:, i], ACT.Exp, scale=-1.0).then_inc(sig["e_out"], 1)
                elif name == "ln":
                    for h in range(NH):
                        act.wait_ge(sig["e_out"], b.of(NH, h + 1))
                        go(cv[:, h], ab[:, h], ACT.Ln, bias=1.0).then_inc(sig["sp"], 1)

            def f_step(step, b, par):
                g = "F"
                name, i = step
                if (g, name) not in NO_BANK:
                    filled(act, g, step, b)
                    w, fr = bank(g, step), free[g][BANK[g, step]]
                if name == "xs":
                    if i == 0:
                        since(act, ready[g], b.of(len(JOBS[g])))
                    elif i >= 2:
                        filled(act, g, ("h", 4 * i - 5), b)
                    n = min(4, ST - 4 * i) * 128
                    go(xsT[:, i % 2, 0:n], w[:, 0:n], ACT.Copy).then_inc(fr, 1)
                elif name == "h":
                    if i >= 2:
                        filled(act, g, ("t", i - 2), b)
                    go(hs[:, i % 2], w[:], ACT.Relu).then_inc(fr, 1)
                elif name == "t":
                    since(act, sig["usedF"], b.of(ST, i - 1 if i >= 2 else 0))
                    go(hsT[:, i % 2], w[:], ACT.Copy).then_inc(fr, 1)
                elif name == "ye":
                    act.wait_ge(sig["usedF"], b.of(ST, min(4 * i + 4, ST)))
                    since(act, sig["ys_out"], b.of(16 * NG, 16 * i))
                    if i == 0:
                        since(act, sig["s1"], b.of(1))
                    n = min(4, ST - 4 * i)
                    go(ys[:, 0:n], tiles(yps[:])[:, 0:n], ACT.Copy).then_inc(sig["ye"], 1)
                elif name == "silu":
                    act.wait_ge(sig["r1"], b.of(1, 1))
                    go(g1[:], fe[:], ACT.Tanh, scale=0.5).then_inc(sig["siluF_e"], 1)

            def copy_bc(n, b):
                act.wait_ge(sig["B_in"], b.of(NS, n + 1))
                for h in range(NH):
                    since(act, dBu[h], b.of(NS, n - 1))
                go(Bs[:, n % 2], Bps[:], ACT.Copy).then_inc(sig["B_out"], 1)
                act.wait_ge(sig["C_in"], b.of(NS, n + 1))
                since(act, sig["P"], b.of(STEPS, NH * (n - 1)))
                go(Cs[:, n % 2], Cps[:], ACT.Copy).then_inc(sig["C_out"], 1)

            def decay(s, b, par):
                n, h = divmod(s, NH)
                if n == 0:
                    act.wait_ge(sig["du%d" % h], b.of(1, 1))
                since(act, sig["scan"], b.of(STEPS, s - 1))
                go(dA[:, s % 2], delta[:, par, h], ACT.Exp, scale=Aneg[:, h * NS + n:h * NS + n + 1]
                   ).then_inc(sig["dA"], 1)

            def do(g, step, it, par):
                if g in "AH":
                    a_step(g, step, it + AHEAD[g], 1 - par)
                elif g == "F":
                    f_step(step, it, par)

            def body(it, par, groups):
                if "F" in groups:
                    if it.is_(0):
                        copy_bc(0, it)
                    decay(0, it, par)
                    deal = slots(groups)
                    for s in range(STEPS):
                        if s + 1 < STEPS:
                            decay(s + 1, it, par)
                        for g, step in deal[s]:
                            do(g, step, it, par)
                        if s % NH == 0 and s // NH + 1 < NS:
                            copy_bc(s // NH + 1, it)
                        elif s == STEPS - NH and "H" in groups:
                            copy_bc(0, it + 1)
                else:
                    for g, step in ORDER:
                        if g in groups:
                            do(g, step, it, par)

            def decay_rates():
                act.wait_ge(loads["mamba"], 16 * len(LOADS["mamba"]))
                go(Aneg[:], W["alog"][:], ACT.Exp).then_inc(prep_act, 1)

            def prepare():
                act.wait_ge(prep_dve, 5)

            act.wait_ge(loads["small"], 16 * len(LOADS["small"]))
            go(bqs[:], W["bq"][:], ACT.Copy, scale=1.0 / D)
            run(act, body, decay_rates, prepare)

        @block.vector
        def _(dve):
            V = nc.vector
            lk = {}

            def spread8(ap):
                return ap.unsqueeze(2).broadcast_to([128, NT, E])

            def moments(g, x, signal):
                for t in range(NT):
                    last = V.bn_stats(stats[:, t], x[:, t])
                lk[g](last)
                dve.sem_inc(sig["stats"], 1)
                for t in range(NT):
                    last = V.bn_aggr(mv[:, t], stats[:, t])
                last.then_inc(sig[signal], 1)

            def first_max(g, p, m, e, hot):
                lk[g](V.tensor_reduce(m[:], p[:], AX.X, ALU.max))
                lk[g](V.tensor_tensor(e[:], p[:], spread8(m[:]), ALU.is_equal))
                lk[g](V.tensor_tensor(e[:], e[:], tiles8(W["first"]), ALU.mult))
                lk[g](V.tensor_reduce(gr[:], e[:], AX.X, ALU.max))
                lk[g](V.tensor_tensor(hot[:], e[:], spread8(gr[:]), ALU.is_equal))

            def tiles8(t):
                return t[:].rearrange("p (i e) -> p i e", e=E)

            def split_rest(g, step, b, dst, head, signal):
                w = bank(g, step)
                dve.wait_ge(sig[head], b.of(1, 1))
                k = V.tensor_tensor(rest, w[0:96], dst, ALU.subtract)
                k.then_inc(free[g][BANK[g, step]], 1)
                emptied(dve, g, step, b)
                V.tensor_copy(dst[32:64], rest[32:64])
                lk[g](V.tensor_copy(midp[64:96], rest[64:96]))
                V.tensor_tensor(dst[64:96], rest[64:96], midp[64:96], ALU.subtract).then_inc(sig[signal], 1)

            def a_step(g, step, b, par, with_a):
                name, i = step
                fr = free[g][BANK[g, step]] if (g, name) not in NO_BANK else None
                w = bank(g, step) if (g, name) not in NO_BANK else None
                if name == "ln0":
                    since(dve, sig["du1"], b.of(1, -1))
                    dve.wait_ge(sig["x_in"], b.of(16, 16))
                    moments(g, x_in, "mean0")
                    dve.wait_ge(sig["rstd0"], b.of(1, 1))
                    for t in range(NT):
                        last = V.tensor_scalar(xn_tok[:, t], x_in[:, t], mv[:, t, 0:1], rstd[:, t:t + 1],
                                               ALU.subtract, ALU.mult)
                    last.then_inc(sig["xn0"], 1)
                elif name == "v":
                    filled(dve, g, step, b)
                    V.tensor_tensor(v_tok, tiles(w[:]), W["bv"][:].unsqueeze(1).broadcast_to([128, NT, D]), ALU.add
                                    ).then_inc(fr, 1)
                elif name == "s":
                    filled(dve, g, step, b)
                    V.tensor_reduce(nmax[:, i:i + 1], w[:], AX.X, ALU.max, negate=True).then_inc(sig["smax"], 1)
                elif name == "gl":
                    filled(dve, g, step, b)
                    wl = w[:, 0:NT * E].rearrange("p (i e) -> p i e", e=E)
                    lk[g](V.tensor_reduce(gm[:], wl, AX.X, ALU.max))
                    V.tensor_tensor(gt[:], wl, spread8(gm[:]), ALU.subtract).then_inc(sig["g_in"], 1)
                    dve.wait_ge(sig["g_in"], b.of(1, 1))
                    dve.sem_inc(fr, 1)
                elif name == "gate":
                    dve.wait_ge(sig["g_exp"], b.of(1, 1))
                    emptied(dve, g, ("gl", 0), b)
                    lk[g](V.tensor_reduce(gm[:], gp[:], AX.X, ALU.add))
                    lk[g](V.reciprocal(gr[:], gm[:]))
                    lk[g](V.tensor_tensor(gp[:], gp[:], spread8(gr[:]), ALU.mult))
                    first_max(g, gp, gm, eq, oh1)
                    lk[g](V.scalar_tensor_tensor(gt[:], oh1[:], -4.0, gp[:], ALU.mult, ALU.add))
                    first_max(g, gt, gm, eq, oh2)
                    lk[g](V.tensor_tensor(oh1[:], oh1[:], oh2[:], ALU.add))
                    lk[g](V.tensor_tensor(gp[:], gp[:], oh1[:], ALU.mult))
                    lk[g](V.tensor_reduce(gm[:], gp[:], AX.X, ALU.add))
                    lk[g](V.tensor_scalar(gm[:], gm[:], 1e-12, None, ALU.max))
                    lk[g](V.reciprocal(gr[:], gm[:]))
                    for k in range(3):
                        last = V.tensor_tensor(grep[:, :, 32 * k:32 * k + E], gp[:], spread8(gr[:]), ALU.mult)
                    last.then_inc(sig["g_rep"], 1)
                elif name == "gT":
                    split_rest(g, step, b, g3[:], "g_hi", "g_split")
                elif name == "o":
                    filled(dve, g, step, b)
                    since(dve, sig["out"], b.of(16, -32))
                    lk[g](V.reciprocal(rs[:], rsum[:]))
                    V.tensor_tensor(s_tok, tiles(w[:]), rs[:].unsqueeze(2).broadcast_to([128, NT, D]), ALU.mult
                                    ).then_inc(fr, 1)
                elif name == "h" and i % 2 == 0:
                    gate_hidden(dve, V, i, b)
                elif name == "silu":
                    dve.wait_ge(sig["siluA_e"], b.of(1, 1))
                    V.scalar_tensor_tensor(g0T, se, 1.0, facc[:], ALU.add, ALU.mult).then_inc(sig["g0T"], 1)
                elif name == "ft":
                    filled(dve, g, step, b)
                    V.scalar_tensor_tensor(tmp, tiles(w[:]), 0.5, s_tok, ALU.mult, ALU.mult).then_inc(fr, 1)
                    emptied(dve, g, step, b)
                    since(dve, sig["kept"], b.of(16))
                    V.tensor_tensor(x_tok[:], x_in[:], tmp, ALU.add).then_inc(sig["x1"], 1)
                elif name == "ln1":
                    if with_a:
                        filled(dve, "A", ("o", 0), b + 1)
                    dve.wait_ge(sig["x1"], b.of(1, 1))
                    moments(g, x_tok, "mean1")
                    dve.wait_ge(sig["rstd1"], b.of(1, 1))
                    for t in range(NT):
                        last = V.tensor_scalar(xn1_tok[:, par, t], x_tok[:, t], mv[:, t, 0:1], rstd[:, t:t + 1],
                                               ALU.subtract, ALU.mult)
                    last.then_inc(sig["xn1"], 1)
                    dve.wait_ge(sig["xn1"], b.of(1, 1))
                    for t in range(NT):
                        last = V.tensor_scalar(ht_tok[:, t], xn1_tok[:, par, t], rstd2[:, t:t + 1], None, ALU.mult)
                    last.then_inc(sig["ht"], 1)
                    lk[g](V.memset(xpad[:, :, 0:TAPS - 1], 0.0))
                elif name == "xi":
                    emptied(dve, g, step, b)
                    cw = W["conv_w"]
                    lk[g](V.tensor_scalar(cv[:, i], xpad[:, i, 0:T], cw[:, i * TAPS:i * TAPS + 1],
                                          W["conv_b"][:, i:i + 1], ALU.mult, ALU.add))
                    for k in range(1, TAPS):
                        last = V.scalar_tensor_tensor(cv[:, i], xpad[:, i, k:k + T],
                                                      cw[:, i * TAPS + k:i * TAPS + k + 1], cv[:, i],
                                                      ALU.mult, ALU.add)
                        if k < TAPS - 1:
                            lk[g](last)
                    last.then_inc(sig["cv"], 1)
                elif name == "z":
                    dve.wait_ge(sig["ec"], b.of(NH, i + 1))
                    V.scalar_tensor_tensor(u[:, par, i], ec[:, i], 1.0, cv[:, i], ALU.add, ALU.mult
                                           ).then_inc(sig["u"], 1)
                    emptied(dve, g, step, b)
                    V.scalar_tensor_tensor(zg[:, par, i], ez[:, i], 1.0, zr[:, i], ALU.add, ALU.mult
                                           ).then_inc(sig["zg"], 1)
                elif name == "bc":
                    split_rest(g, step, b, bc3[:, par], "bc_hi", "bc3")
                elif name == "sc":
                    filled(dve, g, step, b)
                    wl = w[:, 0:NT * E].rearrange("p (i e) -> p i e", e=E)
                    first_max(g, wl, am, eq, ohr)
                    dve.sem_inc(free[g][BANK[g, step]], 1)
                    V.tensor_copy(ohb[:], ohr[:]).then_inc(sig["hot"], 1)
                    dve.wait_ge(sig["a_exp"], b.of(1, 1))
                    lk[g](V.tensor_scalar(alpha[:, par], alpha[:, par], 1.0, None, ALU.add))
                    V.reciprocal(alpha[:, par], alpha[:, par]).then_inc(sig["alpha"], 1)
                elif name == "rk":
                    filled(dve, g, step, b)
                    before, count = w[:, 0:NT * E].rearrange("p (i e) -> p i e", e=E), w[:, NT * E:(NT + 1) * E]
                    lk[g](V.tensor_tensor(more[:], count.unsqueeze(2).broadcast_to([128, E, 4]),
                                          W["full"][:].unsqueeze(1).broadcast_to([128, E, 4]), ALU.is_gt))
                    lk[g](V.tensor_reduce(ntile[:], more[:], AX.X, ALU.add))
                    lk[g](V.tensor_tensor_scan(endt[:], ones8[:], ntile[:], 0.0, ALU.mult, ALU.add))
                    lk[g](V.tensor_tensor(upto[:], endt[0:1].unsqueeze(1).broadcast_to([1, ST, E]),
                                          W["tile_no"][:].unsqueeze(2).broadcast_to([1, ST, E]), ALU.is_le))
                    V.tensor_tensor(endt[:], endt[:], ntile[:], ALU.subtract)
                    lk[g](V.tensor_reduce(texf[:], upto[:], AX.X, ALU.add))
                    V.tensor_scalar(texp[:, par], texf[:], E - 1.0, None, ALU.min)
                    lk[g](V.scalar_tensor_tensor(posr[:], endt[:].unsqueeze(1).broadcast_to([128, NT, E]), 128.0,
                                                 before, ALU.mult, ALU.add))
                    dve.sem_inc(free[g][BANK[g, step]], 1)
                    lk[g](V.tensor_tensor(posr[:], posr[:], ohr[:], ALU.mult))
                    lk[g](V.tensor_reduce(posf[:], posr[:], AX.X, ALU.add))
                    V.tensor_copy(pos[:, par], posf[:]).then_inc(sig["pos"], 1)
                elif name == "dl":
                    dve.wait_ge(sig["e_out"], b.of(NH, i + 1))
                    lk[g](V.tensor_scalar(ez[:, i], ab[:, i], 1.0, -1.0, ALU.add, ALU.add))
                    lk[g](V.scalar_tensor_tensor(ez[:, i], ez[:, i], -1.0, ab[:, i], ALU.mult, ALU.add))
                    V.tensor_tensor(rl[:, i], rl[:, i], ez[:, i], ALU.add).then_inc(sig["e_kept"], 1)
                elif name == "du" and i == 0:
                    finish_delta(dve, V, lk[g], i, b, par)

            def f_step(step, b, par):
                g = "F"
                name, i = step
                if name == "ft":
                    dve.wait_ge(sig["got"], b.of(16 * NT, 16 * NT))
                    dve.wait_ge(sig["alpha"], b.of(1, 1))
                    for t in range(NT):
                        last = V.scalar_tensor_tensor(fe[:, t], fe[:, t], alpha[:, par, t:t + 1],
                                                      xn1_tok[:, par, t], ALU.mult, ALU.add)
                    last.then_inc(sig["r1"], 1)
                    dve.wait_ge(sig["r1"], b.of(1, 1))
                elif name == "silu":
                    dve.wait_ge(sig["siluF_e"], b.of(1, 1))
                    V.scalar_tensor_tensor(g1[:], g1[:], 1.0, fe[:], ALU.add, ALU.mult).then_inc(sig["g1"], 1)

            def scan(s, b):
                dve.wait_ge(sig["dA"], b.of(STEPS, s + 1))
                dve.wait_ge(dBu[s % NH], b.of(NS, s // NH + 1))
                V.tensor_tensor_scan(st[:, s % 4], dA[:, s % 2], st[:, s % 4], 0.0, ALU.mult, ALU.add
                                     ).then_inc(sig["scan"], 1)

            def add_state(s, b, par):
                n, h = divmod(s, NH)
                dve.wait_ge(sig["P"], b.of(STEPS, s + 1))
                if n == 0:
                    V.scalar_tensor_tensor(y[:, h], u[:, par, h], W["dskip"][:, h:h + 1], st[:, s % 4],
                                           ALU.mult, ALU.add).then_inc(sig["y_sum"], 1)
                else:
                    dve.wait_ge(sig["y_sum"], b.of(STEPS, s - 1))
                    V.tensor_tensor(y[:, h], y[:, h], st[:, s % 4], ALU.add).then_inc(sig["y_sum"], 1)

            def c_step(step, b, par):
                if step[0] == "y":
                    for s in range(STEPS - SUM_LAG, STEPS):
                        add_state(s, b, par)
                    dve.wait_ge(sig["y_sum"], b.of(STEPS, STEPS))
                    V.tensor_tensor(du[:, par], y[:], zg[:, par], ALU.mult).then_inc(sig["yo"], 1)
                elif step[0] == "op":
                    filled(dve, "C", step, b)
                    since(dve, sig["out"], b.of(16))
                    V.tensor_tensor(ot[:], tiles(bank("C", step)[:]), xn1_tok[:, par], ALU.add
                                    ).then_inc(free["C"][BANK["C", step]], 1)
                    emptied(dve, "C", step, b)
                    dve.wait_ge(sig["g1"], b.of(1, 1))
                    V.scalar_tensor_tensor(ot[:], ot[:], 0.5, g1[:], ALU.mult, ALU.mult).then_inc(sig["s1"], 1)

            def do(g, step, it, par, groups):
                if g in "AH":
                    a_step(g, step, it + AHEAD[g], 1 - par, "A" in groups)
                elif g == "F":
                    f_step(step, it, par)
                else:
                    c_step(step, it + -1, 1 - par)

            def body(it, par, groups):
                for g in "AH":
                    lk[g] = Link(dve, "dve", g, it + AHEAD[g])
                if "F" in groups:
                    scan_input(dve, V, 0, it, par)
                    deal = slots(groups)
                    for s in range(STEPS):
                        scan(s, it)
                        if s >= SUM_LAG:
                            add_state(s - SUM_LAG, it, par)
                        for g, step in deal[s]:
                            do(g, step, it, par, groups)
                        if s % NH == 1 and s + 1 < STEPS:
                            scan_input(dve, V, s + 1, it, par)
                else:
                    for g, step in ORDER:
                        if g in groups:
                            do(g, step, it, par, groups)
                for g in "AH":
                    if g in groups:
                        lk[g].end()

            def prepare():
                def own(ins):
                    own.n += 1
                    ins.then_inc(prep_own, 1)
                    dve.wait_ge(prep_own, own.n)
                own.n = 0

                def split(raw, parts, n):
                    own(V.tensor_copy(parts[:], raw))
                    own(V.tensor_tensor(raw, raw, parts[:], ALU.subtract))
                    V.tensor_copy(parts[32:64], raw[32:64])
                    own(V.tensor_copy(midp[64:96, 0:n], raw[64:96]))
                    own(V.tensor_tensor(parts[64:96], raw[64:96], midp[64:96, 0:n], ALU.subtract))

                dve.wait_ge(prep_pe, 1)
                for e in range(E):
                    V.tensor_scalar(W["w1f"][:, e * H1:(e + 1) * H1], W["w1f"][:, e * H1:(e + 1) * H1],
                                    W["gammaT"][:, e:e + 1], None, ALU.mult)
                own(V.tensor_tensor(W["b1r"], yps[0:96], W["b1r"], ALU.add))
                split(W["b1r"], b1p, H1)
                split(W["b2r"], b2p, D)
                dve.sem_inc(prep_dve, 1)
                dve.wait_ge(prep_act, 1)
                V.tensor_scalar(Aneg[:], Aneg[:], -1.0, None, ALU.mult).then_inc(prep_dve, 1)

            def after_first():
                dve.wait_ge(loads["mamba"], 16 * len(LOADS["mamba"]))
                V.tensor_scalar(W["conv_w"][:], W["conv_w"][:], 0.5, None, ALU.mult)
                V.tensor_scalar(W["conv_b"][:], W["conv_b"][:], 0.5, None, ALU.mult)
                V.tensor_scalar(W["winT"][:], W["winT"][:], W["norm_w"][:], None, ALU.mult).then_inc(prep_dve, 1)
                dve.wait_ge(loads["ffn1"], 16 * len(LOADS["ffn1"]))
                V.memset(betaM, 0.0).then_inc(prep_memset, 1)
                dve.wait_ge(prep_memset, 1)
                for k in range(3):
                    for e in range(E):
                        c = e * 96 + 32 * k + e
                        last = V.tensor_copy(betaM[:, c:c + 1], W["betaT"][:, e:e + 1])
                last.then_inc(prep_dve, 1)

            V.memset(neghalf[:], -0.5)
            V.memset(eps[:], EPS)
            V.memset(grep[:], 0.0)
            V.memset(fe[:], 0.0)
            V.memset(ones_b[:], 1.0)
            V.memset(ones8[:], 1.0)
            dve.wait_ge(loads["small"], 16 * len(LOADS["small"]))
            V.tensor_copy(sel[:], W["rowsel"][:].unsqueeze(2).broadcast_to([96, 32, 128]))
            V.tensor_copy(ident_b[:], ident[:])
            V.tensor_copy(before_b[:], W["before"])
            V.tensor_scalar(mask_b[:], ident[:], -(2.0 ** 126), None, ALU.mult).then_inc(prep_dve, 1)
            run(dve, body, after_first, prepare)

        @block.gpsimd
        def _(pool):
            G = nc.gpsimd
            lk = {}

            def a_step(g, step, b, par):
                name, i = step
                if name in ("ln0", "ln1"):
                    k = name[2]
                    pool.wait_ge(sig["mean" + k], b.of(1, 1))
                    lk[g](G.tensor_tensor(ve[:], mv[:, :, 1], eps[:], ALU.add))
                    last = G.tensor_tensor(rstd[:], ve[:], neghalf[:], ALU.pow)
                    if name == "ln0":
                        last.then_inc(sig["rstd0"], 1)
                    else:
                        lk[g](last)
                        lk[g](G.tensor_tensor(q2[:], rstd[:], rstd[:], ALU.mult))
                        lk[g](G.tensor_tensor(q2[:], q2[:], mv[:, :, 1], ALU.mult))
                        lk[g](G.tensor_tensor(q2[:], q2[:], eps[:], ALU.add))
                        G.tensor_tensor(rstd2[:], q2[:], neghalf[:], ALU.pow).then_inc(sig["rstd1"], 1)
                elif name == "h" and i % 2 == 1:
                    gate_hidden(pool, G, i, b)
                elif name == "put":
                    if i == 0:
                        pool.wait_ge(sig["pos"], b.of(1, 1))
                        if b.is_(0):
                            pool.wait_ge(sig["xs_zero"], 16 * NG)
                        since(pool, sig["xs_ld"], b.of(16 * NG))
                        pool.sem_inc(sig["go"], 1)
                    G.indirect_dma_start(xs_dram.rearrange("i p d -> (i p) d"),
                                         bass.IndirectOffsetOnAxis(pos[:, par, i:i + 1], 0),
                                         xn1_tok[:, par, i], None).then_inc(sig["put"], 16)
                elif name == "du" and i == 1:
                    finish_delta(pool, G, lk[g], i, b, par)

            def f_step(step, b, par):
                g = "F"
                name, i = step
                if name == "get":
                    if i == 0:
                        pool.wait_ge(sig["ys_out"], b.of(16 * NG, 16 * NG))
                        since(pool, sig["g1"], b.of(1))
                        pool.sem_inc(sig["go"], 1)
                    G.indirect_dma_start(fe[:, i], None, ys_dram.rearrange("i p d -> (i p) d"),
                                         bass.IndirectOffsetOnAxis(pos[:, par, i:i + 1], 0)).then_inc(sig["got"], 16)

            def times_c(s, b):
                n, h = divmod(s, NH)
                if h == 0:
                    pool.wait_ge(sig["C_out"], b.of(NS, n + 1))
                pool.wait_ge(sig["scan"], b.of(STEPS, s + 1))
                G.tensor_tensor(st[:, s % 4], st[:, s % 4], Cs[:, n % 2], ALU.mult).then_inc(sig["P"], 1)

            def do(g, step, it, par):
                if g in "AH":
                    a_step(g, step, it + AHEAD[g], 1 - par)
                elif g == "F":
                    f_step(step, it, par)
                elif step[0] == "op":
                    b = it + -1
                    pool.wait_ge(sig["s1"], b.of(1, 1))
                    pool.wait_ge(sig["xr"], b.of(16, 16))
                    G.tensor_tensor(ot[:], ot[:], xr[:], ALU.add).then_inc(sig["ot"], 1)

            def body(it, par, groups):
                for g in "AH":
                    lk[g] = Link(pool, "pool", g, it + AHEAD[g])
                if "F" in groups:
                    deal = slots(groups)
                    for s in range(STEPS):
                        if s % NH == 0:
                            scan_input(pool, G, s + 1, it, par)
                        times_c(s, it)
                        for g, step in deal[s]:
                            do(g, step, it, par)
                else:
                    for g, step in ORDER:
                        if g in groups:
                            do(g, step, it, par)
                for g in "AH":
                    if g in groups:
                        lk[g].end()

            run(pool, body)


def layouts(i):
    def halves(a):
        return a.reshape(NH, 128, -1).transpose(1, 0, 2).reshape(128, -1)

    def three(a):
        return np.concatenate([a, np.zeros((32 - E, a.shape[1]), a.dtype)] * 3, 0)

    xp = i["L1_attn_x_proj_w"]
    bcrows = xp[RANK:]
    bc3 = np.concatenate([bcrows] * 3 + [xp[:RANK]], 0).T
    col = lambda a: a.reshape(-1, 128).T
    return {
        "x": i["L0_attn_x"],
        **CONSTS,
        "wqT": i["L0_attn_Wq"].T, "wkT": i["L0_attn_Wk"].T, "wvT": i["L0_attn_Wv"].T,
        "bq": col(i["L0_attn_bq"]), "bk": col(i["L0_attn_bk"]),
        "bv": np.broadcast_to(i["L0_attn_bv"], (128, D)),
        "gate": i["L0_ffn_gate"],
        "w1a": i["L0_ffn_W1"].transpose(1, 0, 2).reshape(D, -1),
        "b1a": col(i["L0_ffn_b1"]),
        "w2a": i["L0_ffn_W2"].reshape(-1, 128, D).transpose(1, 0, 2).reshape(128, -1),
        "b2a": i["L0_ffn_b2"],
        "norm_w": col(i["L1_attn_norm_w"]),
        "winT": i["L1_attn_in_proj_w"].T,
        "conv_w": halves(i["L1_attn_conv_w"]), "conv_b": col(i["L1_attn_conv_b"]),
        "xpBC": halves(bc3),
        "dtpT": i["L1_attn_dt_proj_w"].T, "dtb": col(i["L1_attn_dt_proj_b"]),
        "alog": halves(i["L1_attn_A_log"]), "dskip": col(i["L1_attn_D"]),
        "woutT": halves(i["L1_attn_out_proj_w"].T),
        "centT": i["L1_ffn_centroids"].T, "gammaT": i["L1_ffn_gamma"].T, "betaT": i["L1_ffn_beta"].T,
        "w1f": i["L1_ffn_W1"].transpose(2, 0, 1).reshape(D, -1),
        "b1r": three(i["L1_ffn_b1"]),
        "w2f": i["L1_ffn_W2"].reshape(E, D, H1 // 128, 128).transpose(3, 0, 2, 1).reshape(128, -1),
        "b2r": three(i["L1_ffn_b2"]),
    }


def kernel(**inputs):
    import concourse.bacc as _bacc
    from concourse.bass_utils import run_bass_kernel_spmd as _run

    nc = _bacc.Bacc("TRN2", target_bir_lowering=False, num_devices=1)
    arrays, ins = {}, {}
    for name, a in layouts({k: np.asarray(v) for k, v in inputs.items()}).items():
        a = np.ascontiguousarray(a)
        arrays[f"in_{name}_dram"] = a
        t = nc.dram_tensor(f"in_{name}_dram", a.shape, mybir.dt.from_np(a.dtype), kind="ExternalInput")
        ins[name] = (t.ap(), list(a.shape))
    out = nc.dram_tensor("out_dram", (NB, T, D), F32, kind="ExternalOutput").ap()
    xs_dram, ys_dram = (nc.dram_tensor(n, (ST, 128, D), F32, kind="Internal").ap() for n in ("xs_dram", "ys_dram"))
    kept_dram = nc.dram_tensor("kept_dram", (2, T, D), F32, kind="Internal").ap()
    build(nc, ins, out, xs_dram, ys_dram, kept_dram)
    r = _run(nc, [arrays], core_ids=[0])
    return r.results[0]["out_dram"]
```
